# Optimizing a Trainium2 kernel written in Bass

```python
import numpy as np
import jax
import jax.numpy as jnp

def _softmax(x, axis=-1):
    return jax.nn.softmax(x, axis=axis)

def _gelu(x):
    return jax.nn.gelu(x, approximate=True)

def _silu(x):
    return jax.nn.silu(x)

def _sigmoid(x):
    return jax.nn.sigmoid(x)

def _layernorm(x, axis=-1, eps=1e-05):
    m = jnp.mean(x, axis=axis, keepdims=True)
    v = jnp.var(x, axis=axis, keepdims=True)
    return (x - m) / jnp.sqrt(v + eps)

def _scatter_add(tgt, idx, src, axis=0):
    return tgt.at[idx].add(src)

def _segment_sum(src, seg, n):
    return jax.ops.segment_sum(src, seg, n)
kernel_name = 'mk_gnn_preln_d2_gnn_r8_3eb3cd'

def setup_inputs(seed: int=0):
    np.random.seed(seed)
    _w = jnp.asarray

    def _rec_inputs():
        import jax
        import jax.numpy as jnp
        _gk = jax.random.key(seed)
        x = -0.0003713 + 1 * jax.random.normal(jax.random.fold_in(_gk, 1), (6250, 128), jnp.float32)
        src = jax.random.randint(jax.random.fold_in(_gk, 2), (100000,), 0, 6250, jnp.int32)
        dst = jnp.minimum((6250 * jax.random.uniform(jax.random.fold_in(_gk, 3), (100000,)) ** 2.0).astype(jnp.int32), 49999)
        _o = jnp.argsort(dst, stable=True)
        src = src[_o]
        dst = dst[_o]
        edge_attr_32 = 0.000189758 + 1.00013 * jax.random.normal(jax.random.fold_in(_gk, 11), (100000, 32), jnp.float32)
        return (x, src, dst, edge_attr_32)
    x, src, dst, edge_attr_32 = _rec_inputs()

    def _L0_gnn_setup():
        import jax, jax.numpy as jnp
        import numpy as np
        N_NODES = 12500
        N_EDGES = 200000
        IN_DIM = 128
        OUT_DIM = 128
        EDGE_DIM = 32
        EPS = 1e-05

        def _layernorm(h, gamma, beta):
            mu = jnp.mean(h, axis=-1, keepdims=True)
            var = jnp.var(h, axis=-1, keepdims=True)
            return (h - mu) * jax.lax.rsqrt(var + EPS) * gamma + beta
        key = jax.random.key(seed)
        ks = jax.random.split(key, 10)
        hid = OUT_DIM * 2
        x = jax.random.normal(ks[0], (N_NODES, IN_DIM), dtype=jnp.float32)
        edge_index = jax.random.randint(ks[1], (2, N_EDGES), 0, N_NODES, dtype=jnp.int64)
        edge_attr = jax.random.normal(ks[2], (N_EDGES, EDGE_DIM), dtype=jnp.float32)
        W1 = jax.random.normal(ks[3], (IN_DIM + EDGE_DIM, hid), dtype=jnp.float32) / np.sqrt(IN_DIM + EDGE_DIM)
        b1 = jnp.zeros((hid,), jnp.float32)
        g1 = jnp.ones((hid,), jnp.float32)
        be1 = jnp.zeros((hid,), jnp.float32)
        W2 = jax.random.normal(ks[4], (hid, OUT_DIM), dtype=jnp.float32) / np.sqrt(hid)
        b2 = jnp.zeros((OUT_DIM,), jnp.float32)
        Wu = jax.random.normal(ks[5], (IN_DIM + OUT_DIM, OUT_DIM), dtype=jnp.float32) / np.sqrt(IN_DIM + OUT_DIM)
        bu = jnp.zeros((OUT_DIM,), jnp.float32)
        gu = jnp.ones((OUT_DIM,), jnp.float32)
        beu = jnp.zeros((OUT_DIM,), jnp.float32)
        return {'x': x, 'edge_index': edge_index, 'edge_attr': edge_attr, 'W1': W1, 'b1': b1, 'g1': g1, 'be1': be1, 'W2': W2, 'b2': b2, 'Wu': Wu, 'bu': bu, 'gu': gu, 'beu': beu}
    _L0_gnn_all = _L0_gnn_setup()
    _L0_gnn_in = {k: v for k, v in _L0_gnn_all.items() if k in ('W1', 'b1', 'g1', 'be1', 'W2', 'b2', 'Wu', 'bu', 'gu', 'beu')}
    del _L0_gnn_all

    def _L1_gnn_setup():
        import jax, jax.numpy as jnp
        import numpy as np
        N_NODES = 12500
        N_EDGES = 200000
        D_IN = 128
        HIDDEN = [128, 128]

        def _xavier(key, shape):
            fan_out, fan_in = shape
            a = np.sqrt(6.0 / (fan_in + fan_out)).astype(np.float32)
            return jax.random.uniform(key, shape, jnp.float32, -a, a)

        def _mean_aggregate(x, src, dst, n_nodes):
            summed = jax.ops.segment_sum(x[src], dst, num_segments=n_nodes)
            cnt = jax.ops.segment_sum(jnp.ones((src.shape[0],), x.dtype), dst, num_segments=n_nodes)
            return summed / jnp.maximum(cnt, 1.0)[:, None]
        key = jax.random.key(seed)
        ks = jax.random.split(key, 6)
        x = jax.random.normal(ks[0], (N_NODES, D_IN), jnp.float32)
        edge_index = jax.random.randint(ks[1], (2, N_EDGES), 0, N_NODES, dtype=jnp.int64)
        W_conv0 = _xavier(ks[2], (HIDDEN[0], D_IN))
        b_conv0 = jnp.zeros((HIDDEN[0],), jnp.float32)
        W_lin0 = _xavier(ks[3], (HIDDEN[0], D_IN))
        b_lin0 = jnp.zeros((HIDDEN[0],), jnp.float32)
        W_conv1 = _xavier(ks[4], (HIDDEN[1], HIDDEN[0]))
        b_conv1 = jnp.zeros((HIDDEN[1],), jnp.float32)
        W_lin1 = _xavier(ks[5], (HIDDEN[1], HIDDEN[0]))
        b_lin1 = jnp.zeros((HIDDEN[1],), jnp.float32)
        return {'x': x, 'edge_index': edge_index, 'W_conv0': W_conv0, 'b_conv0': b_conv0, 'W_lin0': W_lin0, 'b_lin0': b_lin0, 'W_conv1': W_conv1, 'b_conv1': b_conv1, 'W_lin1': W_lin1, 'b_lin1': b_lin1}
    _L1_gnn_all = _L1_gnn_setup()
    _L1_gnn_in = {k: v for k, v in _L1_gnn_all.items() if k in ('W_conv0', 'b_conv0', 'W_lin0', 'b_lin0', 'W_conv1', 'b_conv1', 'W_lin1', 'b_lin1')}
    del _L1_gnn_all
    return {'x': x, 'src': src, 'dst': dst, 'edge_attr_32': edge_attr_32, 'L0_gnn_W1': _L0_gnn_in['W1'], 'L0_gnn_b1': _L0_gnn_in['b1'], 'L0_gnn_g1': _L0_gnn_in['g1'], 'L0_gnn_be1': _L0_gnn_in['be1'], 'L0_gnn_W2': _L0_gnn_in['W2'], 'L0_gnn_b2': _L0_gnn_in['b2'], 'L0_gnn_Wu': _L0_gnn_in['Wu'], 'L0_gnn_bu': _L0_gnn_in['bu'], 'L0_gnn_gu': _L0_gnn_in['gu'], 'L0_gnn_beu': _L0_gnn_in['beu'], 'L1_gnn_W_conv0': _L1_gnn_in['W_conv0'], 'L1_gnn_b_conv0': _L1_gnn_in['b_conv0'], 'L1_gnn_W_lin0': _L1_gnn_in['W_lin0'], 'L1_gnn_b_lin0': _L1_gnn_in['b_lin0'], 'L1_gnn_W_conv1': _L1_gnn_in['W_conv1'], 'L1_gnn_b_conv1': _L1_gnn_in['b_conv1'], 'L1_gnn_W_lin1': _L1_gnn_in['W_lin1'], 'L1_gnn_b_lin1': _L1_gnn_in['b_lin1']}

def reference(x, src, dst, edge_attr_32, L0_gnn_W1, L0_gnn_b1, L0_gnn_g1, L0_gnn_be1, L0_gnn_W2, L0_gnn_b2, L0_gnn_Wu, L0_gnn_bu, L0_gnn_gu, L0_gnn_beu, L1_gnn_W_conv0, L1_gnn_b_conv0, L1_gnn_W_lin0, L1_gnn_b_lin0, L1_gnn_W_conv1, L1_gnn_b_conv1, L1_gnn_W_lin1, L1_gnn_b_lin1):
    import jax
    import jax.numpy as jnp

    def _L0_gnn_ref(x, edge_index, edge_attr, W1, b1, g1, be1, W2, b2, Wu, bu, gu, beu):
        import jax, jax.numpy as jnp
        import numpy as np
        N_NODES = 12500
        N_EDGES = 200000
        IN_DIM = 128
        OUT_DIM = 128
        EDGE_DIM = 32
        EPS = 1e-05

        def _layernorm(h, gamma, beta):
            mu = jnp.mean(h, axis=-1, keepdims=True)
            var = jnp.var(h, axis=-1, keepdims=True)
            return (h - mu) * jax.lax.rsqrt(var + EPS) * gamma + beta
        row, col = (edge_index[0], edge_index[1])
        msg_in = jnp.concatenate([x[row], edge_attr], axis=-1)
        h = msg_in @ W1 + b1
        h = jax.nn.gelu(_layernorm(h, g1, be1), approximate=False)
        msg = h @ W2 + b2
        agg = jax.ops.segment_sum(msg, col, num_segments=x.shape[0])
        u = jnp.concatenate([x, agg], axis=-1) @ Wu + bu
        u = jax.nn.gelu(_layernorm(u, gu, beu), approximate=False)
        return u + x

    def _L1_gnn_ref(x, edge_index, W_conv0, b_conv0, W_lin0, b_lin0, W_conv1, b_conv1, W_lin1, b_lin1):
        import jax, jax.numpy as jnp
        import numpy as np
        N_NODES = 12500
        N_EDGES = 200000
        D_IN = 128
        HIDDEN = [128, 128]

        def _xavier(key, shape):
            fan_out, fan_in = shape
            a = np.sqrt(6.0 / (fan_in + fan_out)).astype(np.float32)
            return jax.random.uniform(key, shape, jnp.float32, -a, a)

        def _mean_aggregate(x, src, dst, n_nodes):
            summed = jax.ops.segment_sum(x[src], dst, num_segments=n_nodes)
            cnt = jax.ops.segment_sum(jnp.ones((src.shape[0],), x.dtype), dst, num_segments=n_nodes)
            return summed / jnp.maximum(cnt, 1.0)[:, None]
        src, dst = (edge_index[0], edge_index[1])
        n = x.shape[0]
        layers = [(W_conv0, b_conv0, W_lin0, b_lin0), (W_conv1, b_conv1, W_lin1, b_lin1)]
        n_convs = len(layers)
        for i, (Wc, bc, Wl, bl) in enumerate(layers):
            agg = _mean_aggregate(x, src, dst, n)
            h = jnp.einsum('nd,od->no', agg, Wc) + bc
            x = jnp.einsum('nd,od->no', x, Wl) + bl + h
            if i != n_convs - 1:
                x = jax.nn.relu(x)
        return x
    edge_index = jnp.stack([src, dst])
    h = jnp.maximum(_layernorm(x, axis=-1), 0.0)
    x = x + _L0_gnn_ref(h, edge_index, edge_attr_32, L0_gnn_W1, L0_gnn_b1, L0_gnn_g1, L0_gnn_be1, L0_gnn_W2, L0_gnn_b2, L0_gnn_Wu, L0_gnn_bu, L0_gnn_gu, L0_gnn_beu)
    h = jnp.maximum(_layernorm(x, axis=-1), 0.0)
    x = x + _L1_gnn_ref(h, edge_index, L1_gnn_W_conv0, L1_gnn_b_conv0, L1_gnn_W_lin0, L1_gnn_b_lin0, L1_gnn_W_conv1, L1_gnn_b_conv1, L1_gnn_W_lin1, L1_gnn_b_lin1)
    return x

_drawn_inputs = setup_inputs


def setup_inputs(seed=0):
    import zlib

    import numpy as np

    out = dict(_drawn_inputs(seed))
    spreads = {'L0_gnn_b1': (0.0, 0.1),
     'L0_gnn_g1': (1.0, 0.2),
     'L0_gnn_be1': (0.0, 0.1),
     'L0_gnn_b2': (0.0, 0.1),
     'L0_gnn_bu': (0.0, 0.734),
     'L0_gnn_gu': (1.0, 0.2),
     'L0_gnn_beu': (0.0, 0.1),
     'L1_gnn_b_conv0': (0.0, 0.1),
     'L1_gnn_b_lin0': (0.0, 0.1),
     'L1_gnn_b_conv1': (0.0, 0.1),
     'L1_gnn_b_lin1': (0.0, 0.1)}
    factors = {}
    for name, (base, spread) in spreads.items():
        noise = np.random.default_rng([zlib.crc32(name.encode()), seed]).standard_normal(out[name].shape)
        drawn = base * np.exp(spread * noise) if base else spread * noise
        out[name] = jnp.asarray(drawn.astype(out[name].dtype))
    for name, factor in factors.items():
        out[name] = (out[name] * factor).astype(out[name].dtype)
    return out
```

```python
from contextlib import ExitStack

import concourse.bass as bass
from concourse import mybir

F32 = mybir.dt.float32
I32 = mybir.dt.int32
ALU = mybir.AluOpType
ACT = mybir.ActivationFunctionType
AX = mybir.AxisListType

P = 128
BANK = 512

NODES = 6250
EDGES = 100000
D = 128
E = 32
HID = 256
EPS = 1e-5

NODE_TILES = -(-NODES // P)
LAST_ROWS = NODES - (NODE_TILES - 1) * P
BATCH = BANK // D
BATCHES = -(-NODE_TILES // BATCH)

GROUP = 4
TILES = -(-EDGES // P)
GROUPS = -(-TILES // GROUP)
LAST_EDGES = EDGES - (TILES - 1) * P
WINDOW = 96
WINDOWS = -(-NODES // WINDOW)
assert WINDOWS * WINDOW <= NODES + WINDOW
NODE_COLS = NODES + WINDOW

SUPER = 4
LAG = SUPER + 1
WIDE = LAG + 2
RING = 3
EDGE_CHUNK = 4
EDGE_CHUNKS = -(-GROUPS // EDGE_CHUNK)
ROUNDS = 3
CONV_ROUNDS = (1, 2)


def tiles_of(g):
    return min(GROUP, TILES - g * GROUP)


def nodes_of(b):
    return min(BATCH, NODE_TILES - b * BATCH)


def edges_of(t):
    return P if t < TILES - 1 else LAST_EDGES


def gathered():
    count, out = [0] * RING, []
    for n in range(ROUNDS * GROUPS):
        count[n % RING] += 16 * tiles_of(n % GROUPS)
        out.append(count[n % RING])
    return out


GATHERED = gathered()


def build(nc, a, out):
    with ExitStack() as ctx:
        def sb(name, shape, dt=F32):
            return ctx.enter_context(nc.sbuf_tensor(name, shape, dt))

        def ps(name, shape):
            return ctx.enter_context(nc.psum_tensor(name, shape, F32))

        def sem(name):
            return ctx.enter_context(nc.semaphore(name))

        table = [nc.dram_tensor("table_mlp", (NODES, HID), F32).ap(),
                 nc.dram_tensor("table_conv0", (NODES, D), F32).ap(),
                 nc.dram_tensor("table_conv1", (NODES, D), F32).ap()]

        x = sb("x", [P, NODE_TILES * D])
        hT = sb("hT", [P, NODE_TILES * P])
        acc = sb("acc", [P, 3, NODE_COLS])
        rows = sb("rows", [P, RING, GROUP, HID])
        wide = [sb(f"wide{i}", [P, GROUP * HID]) for i in range(WIDE)]
        act = [sb(f"act{i}", [P, GROUP * HID]) for i in range(2)]
        onehot = sb("onehot", [P, 2, GROUP, WINDOW])
        edge = sb("edge", [P, 2, EDGE_CHUNK * P])
        src_i = sb("src_i", [P, GROUPS * GROUP], I32)
        dst_f = sb("dst_f", [P, GROUPS * GROUP])
        dst_rel = sb("dst_rel", [P, GROUPS * GROUP])
        lo_hi_col = sb("lo_hi_col", [P, 4])
        base_f = sb("base_f", [P, GROUPS])
        base_i = sb("base_i", [P, GROUPS], I32)
        span_max = sb("span_max", [P, 1])
        span_i = sb("span_i", [P, 1], I32)
        window_lo = sb("window_lo", [P, 1])
        w1a = sb("w1a", [P, HID])
        w1b = sb("w1b", [P, GROUP, HID])
        w2 = sb("w2", [P, 2, D])
        wu = sb("wu", [P, 2, D])
        w_lin = [sb(f"w_lin{i}", [P, D]) for i in range(2)]
        w_conv = [sb(f"w_conv{i}", [P, D]) for i in range(2)]
        b1 = sb("b1", [1, HID])
        b2 = sb("b2", [1, D])
        bu = sb("bu", [1, D])
        b_sum = sb("b_sum", [1, 2, D])
        b_col = sb("b_col", [P, 2])
        b_col_sum = sb("b_col_sum", [P, 1])
        g1 = sb("g1", [P, HID])
        be1 = sb("be1", [P, HID])
        gu = sb("gu", [P, D])
        beu = sb("beu", [P, D])
        ones = sb("ones", [P, P])
        ident = sb("ident", [P, P])
        iota = sb("iota", [P, WINDOW])
        dst_i = wide[5][:, 0:GROUPS * GROUP].bitcast(I32)
        lo_hi = wide[6][:, 0:2 * GROUPS].rearrange("p (i g) -> p i g", i=2)
        span = wide[4][:, 0:GROUPS]
        iota_i = wide[4][:, GROUPS:GROUPS + WINDOW].bitcast(I32)
        b_row = wide[3][0:1, 0:4 * D].rearrange("p (i d) -> p i d", i=4)
        centre = sb("centre", [P, 8])
        sumsq = sb("sumsq", [P, 2, SUPER * GROUP])
        rstd = sb("rstd", [P, 2, SUPER * GROUP])
        newton = sb("newton", [P, SUPER * GROUP])
        guess = sb("guess", [P, SUPER * GROUP], I32)
        st = sb("st", [P, 8, BATCH])

        mm = ps("mm", [P, 4, BANK])
        seg = ps("seg", [P, 2, BANK])
        node = ps("node", [P, 2, BANK])

        s_w = sem("s_w")
        s_idx = sem("s_idx")
        s_x = [sem(f"s_x{i}") for i in range(BATCHES)]
        s_edge = [sem(f"s_edge{i}") for i in range(2)]
        s_rows = [sem(f"s_rows{i}") for i in range(RING)]
        s_table = [[sem(f"s_table{r}_{i}") for i in range(2)] for r in range(ROUNDS)]
        s_out = [sem(f"s_out{i}") for i in range(2)]
        s_const = sem("s_const")
        s_xpad = sem("s_xpad")
        s_wpad = sem("s_wpad")
        s_zero = sem("s_zero")
        s_wc = sem("s_wc")
        s_lohi = sem("s_lohi")
        s_lohiT = sem("s_lohiT")
        s_lohic = sem("s_lohic")
        s_base = sem("s_base")
        s_drel = sem("s_drel")
        link_v = sem("link_v")
        s_xc = [sem(f"s_xc{i}") for i in range(2)]
        s_sq = [sem(f"s_sq{i}") for i in range(2)]
        s_h = [sem(f"s_h{i}") for i in range(2)]
        s_tr = [sem(f"s_tr{i}") for i in range(2)]
        s_hT = [sem(f"s_hT{i}") for i in range(2)]
        s_p = sem("s_p")
        s_pc = sem("s_pc")
        s_aggp = sem("s_aggp")
        s_aggc = sem("s_aggc")
        s_u = sem("s_u")
        s_usq = sem("s_usq")
        s_un = sem("s_un")
        s_ub = sem("s_ub")
        s_ug = sem("s_ug")
        s_rezero = sem("s_rezero")
        s_ew = sem("s_ew")
        s_add = sem("s_add")
        s_square = sem("s_square")
        s_scaled = sem("s_scaled")
        s_biased = sem("s_biased")
        s_gelu = sem("s_gelu")
        s_onehot = [sem(f"s_onehot{r}") for r in range(ROUNDS)]
        s_seg = [sem(f"s_seg{r}") for r in range(ROUNDS)]
        s_flush = [sem(f"s_flush{r}") for r in range(ROUNDS)]
        g_hot = sem("g_hot")
        g_seg = sem("g_seg")
        s_mean = [sem(f"s_mean{i}") for i in range(2)]
        s_z = [sem(f"s_z{i}") for i in range(2)]
        s_hid = sem("s_hid")
        s_zT = sem("s_zT")
        s_x1T = sem("s_x1T")
        s_o = sem("s_o")

        WEIGHT_LOADS = 5 + 3 + 2 + 4 + 3 + 4 + 2 + 1

        def table_rows(t, b):
            n = nodes_of(b)
            r0 = b * BATCH * P
            if b == BATCHES - 1:
                assert n == 1
                return t[r0:NODES, :]
            return t[r0:r0 + n * P, :].rearrange("(t p) d -> p t d", p=P)

        def batch(t, b, width=D):
            return t[:, b * BATCH * width:(b * BATCH + nodes_of(b)) * width]

        def per_node(v, n, width=D):
            return v.unsqueeze(2).to_broadcast([P, n, width])

        def per_feature(v, n):
            return v.unsqueeze(1).to_broadcast([P, n, v.shape[1]])

        def tiles(v, n):
            return v.rearrange("p (t d) -> p t d", t=n)

        block = ctx.enter_context(nc.Block())

        @block.sync
        def _(sp):
            for b in range(BATCHES):
                if b == BATCHES - 1:
                    sp.wait_ge(s_xpad, 1)
                    sp.dma_start(x[0:LAST_ROWS, (NODE_TILES - 1) * D:], table_rows(a["x"], b)).then_inc(s_x[b], 16)
                else:
                    sp.dma_start(tiles(batch(x, b), BATCH), table_rows(a["x"], b)).then_inc(s_x[b], 16)
                if b == 0:
                    w1, n = a["L0_gnn_W1"], 0
                    loads = [(w1a[:, :], w1[0:D, :])]
                    loads += [(w1b[E * q:E * q + E, q, :], w1[D:D + E, :]) for q in range(GROUP)]
                    loads += [(v, a["L0_gnn_" + k].rearrange("(a n) -> a n", a=1))
                              for v, k in ((b1[:, :], "b1"), (b2[:, :], "b2"), (bu[:, :], "bu"))]
                    loads += [(w2[:, :, :], a["L0_gnn_W2"].rearrange("(h p) n -> p h n", p=P)),
                              (wu[:, :, :], a["L0_gnn_Wu"].rearrange("(h p) n -> p h n", p=P))]
                    loads += [(v[:, :], a["L0_gnn_" + k].partition_broadcast(P))
                              for v, k in ((g1, "g1"), (be1, "be1"), (gu, "gu"), (beu, "beu"))]
                    loads += [(w_lin[0][:, :], a["W_lin0_T"]), (w_conv[0][:, :], a["W_conv0_T"]), (w_lin[1][:, :], a["W_lin1_T"])]
                    loads += [(b_row[:, i, :], a["L1_gnn_b_" + k].rearrange("(a n) -> a n", a=1))
                              for i, k in enumerate(("conv0", "lin0", "conv1", "lin1"))]
                    loads += [(b_col[:, i:i + 1], a["L1_gnn_b_" + k].rearrange("(p a) -> p a", a=1))
                              for i, k in enumerate(("conv0", "lin0"))]
                    loads += [(w_conv[1][:, :], a["W_conv1_T"])]
                    sp.wait_ge(s_wpad, 1)
                    for v, w in loads:
                        sp.dma_start(v, w).then_inc(s_w, 16)
                        n += 1
                    assert n == WEIGHT_LOADS, n
            sp.dma_start(src_i[:, :], a["src"]).then_inc(s_idx, 16)
            sp.dma_start(dst_i[:, :], a["dst"]).then_inc(s_idx, 16)

            def load_edges(c):
                if c >= 2:
                    sp.wait_ge(s_ew, EDGE_CHUNK * (c - 1))
                sp.dma_start(edge[:, c % 2, :], a["edge"][:, c * EDGE_CHUNK * P:(c + 1) * EDGE_CHUNK * P])\
                  .then_inc(s_edge[c % 2], 16)

            load_edges(0)
            load_edges(1)
            for b in range(BATCHES):
                sp.wait_ge(s_pc, b + 1)
                v = wide[b % 2][:, 0:nodes_of(b) * HID]
                if b < BATCHES - 1:
                    v = tiles(v, BATCH)
                else:
                    v = v[0:LAST_ROWS, :]
                sp.dma_start(table_rows(table[0], b), v).then_inc(s_table[0][b % 2], 16)
            for c in range(2, EDGE_CHUNKS):
                load_edges(c)
            for b in range(BATCHES):
                sp.wait_ge(s_h[1], b + 1)
                v = act[b % 2][:, BANK:BANK + nodes_of(b) * D]
                v = tiles(v, BATCH) if b < BATCHES - 1 else v[0:LAST_ROWS, :]
                sp.dma_start(table_rows(table[1], b), v).then_inc(s_table[1][b % 2], 16)
            for b in range(BATCHES):
                sp.wait_ge(s_hid, b + 1)
                v = wide[b % 2][:, 0:nodes_of(b) * D]
                v = tiles(v, BATCH) if b < BATCHES - 1 else v[0:LAST_ROWS, :]
                sp.dma_start(table_rows(table[2], b), v).then_inc(s_table[2][b % 2], 16)
            for b in range(BATCHES):
                sp.wait_ge(s_o, b + 1)
                v = act[b % 2][:, 0:nodes_of(b) * D]
                v = tiles(v, BATCH) if b < BATCHES - 1 else v[0:LAST_ROWS, :]
                sp.dma_start(table_rows(out, b), v).then_inc(s_out[b % 2], 16)
            for i in range(2):
                sp.wait_ge(s_out[i], 16 * len(range(i, BATCHES, 2)))

        @block.gpsimd
        def _(pool):
            pool.memset(w1b[:, :, :], 0.0).then_inc(s_wpad, 1)
            pool.memset(x[:, (NODE_TILES - 1) * D:], 0.0).then_inc(s_xpad, 1)
            pool.memset(ident[:, :], 0.0).then_inc(s_const, 1)
            pool.memset(ones[:, :], 1.0).then_inc(s_const, 1)
            pool.iota(iota_i[:, :], pattern=[[1, WINDOW]], base=0, channel_multiplier=0).then_inc(s_const, 1)
            pool.wait_ge(s_const, 3)
            pool.affine_select(out=ident[:, :], in_=ident[:, :], compare_op=ALU.not_equal, fill=1.0,
                               base=0, pattern=[[-1, P]], channel_multiplier=1).then_inc(s_const, 1)
            pool.memset(acc[:, :, :], 0.0).then_inc(s_zero, 1)
            pool.wait_ge(s_idx, 32)
            for r in range(ROUNDS):
                if r == 1:
                    for b in range(BATCHES):
                        pool.wait_ge(s_aggp, b + 1)
                        pool.memset(acc[:, 0:2, b * BANK:min((b + 1) * BANK, NODE_COLS)], 0.0).then_inc(s_rezero, 1)
                for i in range(2):
                    pool.wait_ge(s_table[r][i], 16 * len(range(i, BATCHES, 2)))
                width = HID if r == 0 else D
                for g in range(GROUPS):
                    n = r * GROUPS + g
                    if g >= RING:
                        if r == 0:
                            pool.wait_ge(s_add, g - RING + 1)
                        else:
                            pool.wait_ge(s_seg[r], g - RING + 1)
                    for q in range(tiles_of(g)):
                        t = g * GROUP + q
                        pool.indirect_dma_start(rows[:, n % RING, q, 0:width], None, table[r],
                                                bass.IndirectOffsetOnAxis(ap=src_i[:, t:t + 1], axis=0))\
                            .then_inc(s_rows[n % RING], 16)

        @block.tensor
        def _(pe):
            def transposes(phase, b):
                pe.wait_ge(s_h[phase], b + 1)
                if b >= 2:
                    pe.wait_ge(s_hT[phase], b - 1)
                n = nodes_of(b)
                for j in range(n):
                    v = act[b % 2][:, BANK + j * D:BANK + (j + 1) * D]
                    last = pe.transpose(seg[:, b % 2, j * P:(j + 1) * P], v, ident[:, :])
                last.then_inc(s_tr[phase], 1)

            def mlp_table(b):
                pe.wait_ge(s_hT[0], b + 1)
                if b >= 2:
                    pe.wait_ge(s_pc, b - 1)
                for j in range(nodes_of(b)):
                    o = mm[:, 2 * (b % 2) + j // 2, (j % 2) * HID:(j % 2 + 1) * HID]
                    c = (b * BATCH + j) * P
                    pe.matmul(o, hT[:, c:c + P], w1a[:, :], start=True, stop=False)
                    last = pe.matmul(o, ones[0:1, :], b1[:, :], start=False, stop=True)
                last.then_inc(s_p, 1)

            pe.wait_ge(s_const, 4)
            for b in range(BATCHES + 1):
                if b < BATCHES:
                    transposes(0, b)
                if b == 1:
                    pe.wait_ge(s_wc, 1)
                if b >= 1:
                    mlp_table(b - 1)

            half = GROUPS // 2
            pe.wait_ge(s_lohi, 1)
            for i in range(4):
                last = pe.transpose(node[0:half, 0, i * P:(i + 1) * P],
                                    lo_hi[:, i // 2, (i % 2) * half:(i % 2 + 1) * half], ident[:, :])
            last.then_inc(s_lohiT, 1)
            pe.wait_ge(s_lohic, 1)
            for i in range(4):
                last = pe.matmul(node[:, 1, i * half:(i + 1) * half], wide[2][0:half, i * P:(i + 1) * P],
                                 ident[0:half, 0:half], start=True, stop=True)
            last.then_inc(s_base, 1)

            def edge_part(g):
                c = g // EDGE_CHUNK
                pe.wait_ge(s_edge[c % 2], 16 * (c // 2 + 1))
                if g >= 2:
                    pe.wait_ge(s_add, g - 1)
                col = (g % EDGE_CHUNK) * P
                for q in range(tiles_of(g)):
                    last = pe.matmul(mm[:, 2 * (g % 2) + q // 2, (q % 2) * HID:(q % 2 + 1) * HID],
                                     edge[:, c % 2, col:col + P], w1b[:, q, :], start=True, stop=True)
                last.then_inc(s_ew, 1)

            def window_sums(r, g):
                n, nt = r * GROUPS + g, tiles_of(g)
                parts = [2, 0, 1] if r == 0 else [0]
                for h in parts:
                    for q in range(nt):
                        k = edges_of(g * GROUP + q)
                        if h == 2:
                            v = ones[0:k, :]
                        elif r == 0:
                            v = act[g % 2][0:k, q * HID + h * D:q * HID + (h + 1) * D]
                        else:
                            v = rows[0:k, n % RING, q, 0:D]
                        last = pe.matmul(seg[:, g % 2, h * WINDOW:(h + 1) * WINDOW], v,
                                         onehot[0:k, g % 2, q, :], start=(q == 0), stop=(q == nt - 1))
                return last

            def segment(r, g, general):
                n = r * GROUPS + g
                if g >= 2:
                    pe.wait_ge(s_flush[r], g - 1)
                if r == 0:
                    pe.wait_ge(s_gelu, g + 1)
                else:
                    pe.wait_ge(s_rows[n % RING], GATHERED[n])
                if not general:
                    pe.wait_ge(s_onehot[r], g + 1)
                    window_sums(r, g).then_inc(s_seg[r], 1)
                    return
                with pe.Fori(0, WINDOWS):
                    pe.wait_ge(g_hot, 1)
                    pe.sem_clear(g_hot)
                    window_sums(r, g).then_inc(g_seg, 1)
                pe.drain().then_inc(s_seg[r], 1)

            def mlp_round(general):
                pe.wait_ge(s_pc, BATCHES)
                for i in range(GROUPS + LAG + 1):
                    if i < GROUPS:
                        edge_part(i)
                    if i > LAG:
                        segment(0, i - LAG - 1, general)

            def node_update():
                def aggregate(b):
                    n, c = nodes_of(b), b * BANK
                    o = node[:, b % 2, 0:n * P]
                    if b >= 2:
                        pe.wait_ge(s_aggc, b - 1)
                    pe.matmul(o, w2[:, 0, :], acc[:, 0, c:c + n * P], start=True, stop=False)
                    pe.matmul(o, w2[:, 1, :], acc[:, 1, c:c + n * P], start=False, stop=False)
                    pe.matmul(o, b2[:, :], acc[0:1, 2, c:c + n * P], start=False, stop=True).then_inc(s_aggp, 1)

                def update(b):
                    pe.wait_ge(s_aggc, b + 1)
                    if b >= 4:
                        pe.wait_ge(s_un, b - 3)
                    for j in range(nodes_of(b)):
                        o = mm[:, b % 4, j * D:(j + 1) * D]
                        c = (b * BATCH + j) * P
                        pe.matmul(o, hT[:, c:c + P], wu[:, 0, :], start=True, stop=False)
                        pe.matmul(o, wide[b % 2][:, j * P:(j + 1) * P], wu[:, 1, :], start=False, stop=False)
                        last = pe.matmul(o, ones[0:1, :], bu[:, :], start=False, stop=True)
                    last.then_inc(s_u, 1)

                pe.wait_ge(s_flush[0], GROUPS)
                for b in range(BATCHES + 4):
                    if b < BATCHES:
                        aggregate(b)
                    if 1 <= b < BATCHES + 1:
                        update(b - 1)
                    if b >= 4:
                        transposes(1, b - 4)

            def conv_rows(i, b):
                pe.wait_ge(s_mean[i], b + 1)
                if b >= 2:
                    if i == 0:
                        pe.wait_ge(s_hid, b - 1)
                    else:
                        pe.wait_ge(s_o, b - 1)
                for j in range(nodes_of(b)):
                    o = node[:, b % 2, j * D:(j + 1) * D]
                    c = (b * BATCH + j) * P
                    pe.matmul(o, hT[:, c:c + P], w_lin[i][:, :], start=True, stop=False)
                    pe.matmul(o, acc[:, i, c:c + P], w_conv[i][:, :], start=False, stop=False)
                    last = pe.matmul(o, ones[0:1, :], b_sum[:, i, :], start=False, stop=True)
                last.then_inc(s_z[i], 1)

            def hidden_columns(b):
                n, c = nodes_of(b), b * BANK
                o = mm[:, b % 4, 0:n * P]
                if b >= 4:
                    pe.wait_ge(s_x1T, b - 3)
                pe.matmul(o, w_lin[0][:, :], hT[:, c:c + n * P], start=True, stop=False)
                pe.matmul(o, w_conv[0][:, :], acc[:, 0, c:c + n * P], start=False, stop=True).then_inc(s_zT, 1)

            def conv_round(r, general):
                if r == 1:
                    pe.wait_ge(s_hT[1], BATCHES)
                for g in range(GROUPS):
                    segment(r, g, general)
                    if r == 2 and 1 <= g <= BATCHES:
                        hidden_columns(g - 1)

            def rounds(general):
                mlp_round(general)
                node_update()
                conv_round(1, general)
                for b in range(BATCHES):
                    conv_rows(0, b)
                conv_round(2, general)
                pe.wait_ge(s_x1T, BATCHES)
                for b in range(BATCHES):
                    conv_rows(1, b)

            pe.wait_ge(s_drel, 1)
            widest = pe.value_load(span_i[0:1, 0:1], min_val=0, max_val=NODES)
            with pe.If(widest >= WINDOW):
                rounds(True)
            with pe.Else():
                rounds(False)

        @block.scalar
        def _(ac):
            def square(phase, b):
                n = nodes_of(b)
                ac.wait_ge(s_xc[phase], b + 1)
                ac.activation(act[b % 2][:, 0:n * D] if phase == 0 else wide[2][:, 0:n * D],
                              wide[2][:, (b % 2) * BANK:(b % 2) * BANK + n * D] if phase == 0
                              else act[b % 2][:, BANK:BANK + n * D], ACT.Square).then_inc(s_sq[phase], 1)

            def copy_hT(phase, b):
                n = nodes_of(b)
                ac.wait_ge(s_tr[phase], b + 1)
                ac.activation(hT[:, b * BANK:b * BANK + n * P], seg[:, b % 2, 0:n * P], ACT.Copy).then_inc(s_hT[phase], 1)

            def copy_table(b):
                n = nodes_of(b)
                ac.wait_ge(s_p, b + 1)
                if b >= 2:
                    ac.wait_ge(s_table[0][b % 2], 16 * (b // 2))
                for i in range(0, n, 2):
                    k = min(2, n - i) * HID
                    last = ac.activation(wide[b % 2][:, i * HID:i * HID + k], mm[:, 2 * (b % 2) + i // 2, 0:k], ACT.Copy)
                last.then_inc(s_pc, 1)

            for b in range(BATCHES + 2):
                if b < BATCHES:
                    square(0, b)
                if 1 <= b <= BATCHES:
                    copy_hT(0, b - 1)
                if b >= 2:
                    copy_table(b - 2)

            for i in range(GROUPS + LAG):
                if i < GROUPS:
                    ac.wait_ge(s_add, i + 1)
                    if i >= 1:
                        ac.wait_ge(s_square, i)
                    for q in range(tiles_of(i)):
                        v = wide[i % WIDE][:, q * HID:(q + 1) * HID]
                        t = (i % SUPER) * GROUP + q
                        last = ac.activation(act_junk(node, q), v, ACT.Square, accum_out=sumsq[:, i // SUPER % 2, t:t + 1])
                    last.then_inc(s_square, 1)
                g = i - LAG
                if g >= 0:
                    k = tiles_of(g) * HID
                    ac.wait_ge(s_biased, g + 1)
                    if g >= 2:
                        ac.wait_ge(s_seg[0], g - 1)
                    ac.activation(act[g % 2][:, 0:k], wide[g % WIDE][:, 0:k], ACT.Gelu).then_inc(s_gelu, 1)

            ac.wait_ge(s_seg[0], GROUPS)
            def copy_agg(b):
                n = nodes_of(b)
                ac.wait_ge(s_aggp, b + 1)
                if b >= 2:
                    ac.wait_ge(s_u, b - 1)
                ac.activation(wide[b % 2][:, 0:n * P], node[:, b % 2, 0:n * P], ACT.Copy).then_inc(s_aggc, 1)

            def square_u(b):
                n = nodes_of(b)
                ac.wait_ge(s_u, b + 1)
                if b >= 2:
                    ac.wait_ge(s_un, b - 1)
                ac.activation(wide[b % 2][:, BANK:BANK + n * D], mm[:, b % 4, 0:n * D], ACT.Square).then_inc(s_usq, 1)

            def gelu_u(b):
                n = nodes_of(b)
                ac.wait_ge(s_ub, b + 1)
                ac.activation(act[b % 2][:, 0:n * D], act[b % 2][:, 0:n * D], ACT.Gelu).then_inc(s_ug, 1)

            for b in range(BATCHES + 5):
                if b < BATCHES:
                    copy_agg(b)
                if 1 <= b < BATCHES + 1:
                    square_u(b - 1)
                if 2 <= b < BATCHES + 2:
                    gelu_u(b - 2)
                if 3 <= b < BATCHES + 3:
                    square(1, b - 3)
                if b >= 5:
                    copy_hT(1, b - 5)

            for b in range(BATCHES):
                n = nodes_of(b)
                ac.wait_ge(s_z[0], b + 1)
                if b >= 2:
                    ac.wait_ge(s_table[2][b % 2], 16 * (b // 2))
                ac.activation(wide[b % 2][:, 0:n * D], node[:, b % 2, 0:n * D], ACT.Relu).then_inc(s_hid, 1)
            for b in range(BATCHES):
                n = nodes_of(b)
                ac.wait_ge(s_zT, b + 1)
                ac.activation(hT[:, b * BANK:b * BANK + n * P], mm[:, b % 4, 0:n * P], ACT.Relu,
                              bias=b_col_sum[:, 0:1]).then_inc(s_x1T, 1)

        @block.vector
        def _(ve):
            linked = [0]

            def link(ins):
                linked[0] += 1
                ins.then_inc(link_v, 1)
                ve.wait_ge(link_v, linked[0])

            def tt(o, i0, i1, op):
                return ve.tensor_tensor(o, i0, i1, op)

            def ts(o, i0, s1, s2, op0, op1=None):
                return ve.tensor_scalar(o, i0, s1, s2, op0, op1) if op1 is not None else ve.tensor_scalar(o, i0, s1, None, op0)

            ve.wait_ge(s_w, 16 * WEIGHT_LOADS)
            for w, k, n in ((w1a, P, HID), (w1b, P, HID), (b1, 1, HID), (wu, P, D), (bu, 1, D)):
                for v in ([w[:, i, :] for i in range(w.shape[1])] if len(w.shape) == 3 else [w[:, :]]):
                    link(ve.tensor_reduce(centre[0:k, 0:1], v, AX.X, ALU.add))
                    link(ts(centre[0:k, 1:2], centre[0:k, 0:1], -1.0 / n, None, ALU.mult))
                    link(ts(v, v, centre[0:k, 1:2], None, ALU.add))
            link(ts(g1[:, :], g1[:, :], float(HID) ** 0.5, None, ALU.mult))
            for i in range(2):
                link(tt(b_sum[:, i, :], b_row[:, 2 * i, :], b_row[:, 2 * i + 1, :], ALU.add))
            tt(b_col_sum[:, :], b_col[:, 0:1], b_col[:, 1:2], ALU.add).then_inc(s_wc, 1)

            def centre_x(phase, b, xc):
                n = nodes_of(b)
                xb = tiles(batch(x, b), n)
                link(ve.tensor_reduce(st[:, 0, 0:n], xb, AX.X, ALU.add))
                link(ts(st[:, 1, 0:n], st[:, 0, 0:n], -1.0 / D, None, ALU.mult))
                tt(tiles(xc, n), xb, per_node(st[:, 1, 0:n], n), ALU.add).then_inc(s_xc[phase], 1)

            def inverse_root(y, v, n):
                gi, t = guess[:, 0:n], newton[:, 0:n]
                link(ts(gi, v.bitcast(I32), 1, None, ALU.logical_shift_right))
                link(ts(gi, gi, -1.0, float(0x5F3759DF), ALU.mult, ALU.add))
                g = gi.bitcast(F32)
                for _ in range(3):
                    link(tt(t, g, g, ALU.mult))
                    link(ve.scalar_tensor_tensor(out=t, in0=t, scalar=-0.5, in1=v, op0=ALU.mult, op1=ALU.mult))
                    link(ve.scalar_tensor_tensor(out=y, in0=t, scalar=1.5, in1=g, op0=ALU.add, op1=ALU.mult))
                    g = y

            def inverse_deviation(o, i, n):
                link(ts(i, i, 1.0 / D, EPS, ALU.mult, ALU.add))
                inverse_root(o, i, n)

            def phase0_first(b):
                n = nodes_of(b)
                ve.wait_ge(s_x[b], 16)
                if b >= 2:
                    ve.wait_ge(s_h[0], b - 1)
                centre_x(0, b, wide[2][:, (b % 2) * BANK:(b % 2) * BANK + n * D])

            def phase0_second(b):
                n = nodes_of(b)
                xb = tiles(batch(x, b), n)
                xc = tiles(wide[2][:, (b % 2) * BANK:(b % 2) * BANK + n * D], n)
                h = tiles(act[b % 2][:, BANK:BANK + n * D], n)
                ve.wait_ge(s_sq[0], b + 1)
                link(ve.tensor_reduce(st[:, 2, 0:n], tiles(act[b % 2][:, 0:n * D], n), AX.X, ALU.add))
                inverse_deviation(st[:, 3, 0:n], st[:, 2, 0:n], n)
                if b >= 2:
                    ve.wait_ge(s_tr[0], b - 1)
                ve.scalar_tensor_tensor(out=h, in0=xc, scalar=0.0, in1=per_node(st[:, 3, 0:n], n),
                                        op0=ALU.max, op1=ALU.mult).then_inc(s_h[0], 1)
                ve.wait_ge(s_h[0], b + 1)
                link(tt(xb, xb, h, ALU.add))

            for b in range(BATCHES + 1):
                if b < BATCHES:
                    phase0_first(b)
                if b >= 1:
                    phase0_second(b - 1)

            ve.wait_ge(s_idx, 32)
            link(ve.tensor_copy(dst_f[:, :], dst_i[:, :]))
            by_group = dst_f[:, :].rearrange("p (g q) -> p g q", q=GROUP)
            ve.tensor_reduce(lo_hi[:, 0, :], by_group, AX.X, ALU.min)
            ve.tensor_reduce(lo_hi[:, 1, :], by_group, AX.X, ALU.max).then_inc(s_lohi, 1)
            ve.wait_ge(s_lohiT, 1)
            half = GROUPS // 2
            v = node[0:half, 0, :].rearrange("p (i c) -> p i c", i=4)
            ve.tensor_reduce(lo_hi_col[0:half, 0:2], v[:, 0:2, :], AX.X, ALU.min)
            link(ve.tensor_reduce(lo_hi_col[0:half, 2:4], v[:, 2:4, :], AX.X, ALU.max))
            ve.wait_ge(s_h[0], BATCHES)
            ve.tensor_copy(wide[2][0:half, 0:4 * P].rearrange("p (i c) -> p i c", i=4),
                           lo_hi_col[0:half, :].unsqueeze(2).to_broadcast([half, 4, P])).then_inc(s_lohic, 1)
            ve.wait_ge(s_base, 1)
            link(ve.tensor_copy(base_f[:, :], node[:, 1, 0:GROUPS]))
            link(ve.tensor_copy(base_i[:, :], base_f[:, :]))
            link(tt(span[:, :], node[:, 1, GROUPS:2 * GROUPS], base_f[:, :], ALU.subtract))
            link(ve.tensor_reduce(span_max[:, :], span[:, :], AX.X, ALU.max))
            link(ve.tensor_copy(span_i[:, :], span_max[:, :]))
            ve.wait_ge(s_const, 4)
            link(ve.tensor_copy(iota[:, :], iota_i[:, :]))
            tt(dst_rel[:, :].rearrange("p (g q) -> p g q", q=GROUP), by_group,
               base_f[:, :].unsqueeze(2).to_broadcast([P, GROUPS, GROUP]), ALU.subtract).then_inc(s_drel, 1)
            ve.wait_ge(s_drel, 1)

            def hot(r, g, general):
                if general:
                    return
                if g >= 2:
                    ve.wait_ge(s_seg[r], g - 1)
                for q in range(tiles_of(g)):
                    t = g * GROUP + q
                    last = ts(onehot[:, g % 2, q, :], iota[:, :], dst_rel[:, t:t + 1], None, ALU.is_equal)
                last.then_inc(s_onehot[r], 1)

            def add_window(r, g, start):
                parts = slice(0, 3) if r == 0 else slice(r - 1, r)
                n = 3 if r == 0 else 1
                o = acc[:, parts, bass.ds(start, WINDOW)]
                return tt(o, o, seg[:, g % 2, 0:n * WINDOW].rearrange("p (h w) -> p h w", h=n), ALU.add)

            def flush(r, g, general):
                if not general:
                    start = ve.value_load(base_i[0:1, g:g + 1], min_val=0, max_val=NODES - 1)
                    ve.wait_ge(s_seg[r], g + 1)
                    if g >= 1:
                        ve.wait_ge(s_flush[r], g)
                    add_window(r, g, start).then_inc(s_flush[r], 1)
                    return
                ve.memset(window_lo[:, :], 0.0)
                with ve.Fori(0, WINDOWS) as w:
                    ve.drain()
                    for q in range(tiles_of(g)):
                        t = g * GROUP + q
                        last = ts(onehot[:, g % 2, q, :], iota[:, :], window_lo[:, 0:1], dst_f[:, t:t + 1],
                                  ALU.add, ALU.is_equal)
                    last.then_inc(g_hot, 1)
                    ve.wait_ge(g_seg, 1)
                    ve.sem_clear(g_seg)
                    add_window(r, g, w * WINDOW)
                    ts(window_lo[:, :], window_lo[:, :], float(WINDOW), None, ALU.add)
                ve.drain().then_inc(s_flush[r], 1)

            def mlp_round(general):
                def add_nodes(g):
                    ve.wait_ge(s_ew, g + 1)
                    ve.wait_ge(s_rows[g % RING], GATHERED[g])
                    if g >= WIDE:
                        ve.wait_ge(s_gelu, g - WIDE + 1)
                    k = tiles_of(g)
                    for i in range(0, k, 2):
                        o = tiles(wide[g % WIDE][:, i * HID:(i + 2) * HID], 2)
                        last = tt(o, tiles(mm[:, 2 * (g % 2) + i // 2, :], 2), rows[:, g % RING, i:i + 2, :], ALU.add)
                    last.then_inc(s_add, 1)

                def invert(i):
                    first = i * SUPER
                    last = min(first + SUPER, GROUPS) - 1
                    n = (last - first) * GROUP + tiles_of(last)
                    ve.wait_ge(s_square, last + 1)
                    link(ts(sumsq[:, i % 2, 0:n], sumsq[:, i % 2, 0:n], HID * EPS, None, ALU.add))
                    inverse_root(rstd[:, i % 2, 0:n], sumsq[:, i % 2, 0:n], n)

                def normalise(g):
                    k = tiles_of(g)
                    for q in range(k):
                        v = wide[g % WIDE][:, q * HID:(q + 1) * HID]
                        t = (g % SUPER) * GROUP + q
                        last = ve.scalar_tensor_tensor(out=v, in0=v, scalar=rstd[:, g // SUPER % 2, t:t + 1],
                                                       in1=g1[:, :], op0=ALU.mult, op1=ALU.mult)
                    last.then_inc(s_scaled, 1)
                    ve.wait_ge(s_scaled, g + 1)
                    v = tiles(wide[g % WIDE][:, 0:k * HID], k)
                    tt(v, v, per_feature(be1[:, :], k), ALU.add).then_inc(s_biased, 1)

                for g in range(GROUPS + LAG + 1):
                    if g < GROUPS:
                        add_nodes(g)
                    if LAG <= g < GROUPS + LAG:
                        if (g - LAG) % SUPER == 0:
                            invert((g - LAG) // SUPER)
                        normalise(g - LAG)
                        hot(0, g - LAG, general)
                    if g > LAG:
                        flush(0, g - LAG - 1, general)

            def node_update():
                def normalise_u(b):
                    n = nodes_of(b)
                    v = act[b % 2][:, 0:n * D]
                    ve.wait_ge(s_usq, b + 1)
                    link(ve.tensor_reduce(st[:, 4, 0:n], tiles(wide[b % 2][:, BANK:BANK + n * D], n), AX.X, ALU.add))
                    inverse_deviation(st[:, 5, 0:n], st[:, 4, 0:n], n)
                    tt(tiles(v, n), tiles(mm[:, b % 4, 0:n * D], n), per_node(st[:, 5, 0:n], n), ALU.mult).then_inc(s_un, 1)
                    ve.wait_ge(s_un, b + 1)
                    link(tt(tiles(v, n), tiles(v, n), per_feature(gu[:, :], n), ALU.mult))
                    tt(tiles(v, n), tiles(v, n), per_feature(beu[:, :], n), ALU.add).then_inc(s_ub, 1)

                def residual(b):
                    n = nodes_of(b)
                    ve.wait_ge(s_ug, b + 1)
                    link(tt(batch(x, b), batch(x, b), act[b % 2][:, 0:n * D], ALU.add))
                    if b >= 2:
                        ve.wait_ge(s_tr[1], b - 1)
                        ve.wait_ge(s_table[1][b % 2], 16 * (b // 2))
                    centre_x(1, b, act[b % 2][:, BANK:BANK + n * D])

                def second_h(b):
                    n = nodes_of(b)
                    h = tiles(act[b % 2][:, BANK:BANK + n * D], n)
                    ve.wait_ge(s_sq[1], b + 1)
                    link(ve.tensor_reduce(st[:, 6, 0:n], tiles(wide[2][:, 0:n * D], n), AX.X, ALU.add))
                    inverse_deviation(st[:, 7, 0:n], st[:, 6, 0:n], n)
                    ve.scalar_tensor_tensor(out=h, in0=h, scalar=0.0, in1=per_node(st[:, 7, 0:n], n),
                                            op0=ALU.max, op1=ALU.mult).then_inc(s_h[1], 1)

                for b in range(BATCHES + 2):
                    if b < BATCHES:
                        normalise_u(b)
                    if b >= 2:
                        second_h(b - 2)
                    if 1 <= b <= BATCHES:
                        residual(b - 1)

            def conv_round(r, general):
                if r == 1:
                    ve.wait_ge(s_rezero, BATCHES)
                for g in range(GROUPS + 1):
                    if g < GROUPS:
                        hot(r, g, general)
                    if g >= 1:
                        flush(r, g - 1, general)
                    if r == 1 and 1 <= g <= BATCHES:
                        v = acc[:, 2, (g - 1) * BANK:min(g * BANK, NODE_COLS)]
                        link(ts(v, v, 1.0, None, ALU.max))
                        link(ve.reciprocal(v, v))

            def means(i, b):
                v = acc[:, i, b * BANK:b * BANK + nodes_of(b) * P]
                tt(v, v, acc[:, 2, b * BANK:b * BANK + nodes_of(b) * P], ALU.mult).then_inc(s_mean[i], 1)

            def rounds(general):
                mlp_round(general)
                node_update()
                conv_round(1, general)
                for b in range(BATCHES):
                    if b == 0:
                        ve.wait_ge(s_flush[1], GROUPS)
                    means(0, b)
                conv_round(2, general)
                ve.wait_ge(s_flush[2], GROUPS)
                for b in range(BATCHES + 1):
                    if b < BATCHES:
                        means(1, b)
                    if b >= 1:
                        n, c = nodes_of(b - 1), (b - 1) % 2
                        ve.wait_ge(s_z[1], b)
                        if b >= 3:
                            ve.wait_ge(s_out[c], 16 * ((b - 1) // 2))
                        tt(act[c][:, 0:n * D], batch(x, b - 1), node[:, c, 0:n * D], ALU.add).then_inc(s_o, 1)

            ve.wait_ge(s_zero, 1)
            widest = ve.value_load(span_i[0:1, 0:1], min_val=0, max_val=NODES)
            before = linked[0]
            with ve.If(widest >= WINDOW):
                rounds(True)
            linked[0] = before
            with ve.Else():
                rounds(False)


def act_junk(node, q):
    return node[:, q // 2, (q % 2) * HID:(q % 2 + 1) * HID]


_PLAIN = ["x", "L0_gnn_W1", "L0_gnn_b1", "L0_gnn_g1", "L0_gnn_be1", "L0_gnn_W2", "L0_gnn_b2", "L0_gnn_Wu", "L0_gnn_bu",
          "L0_gnn_gu", "L0_gnn_beu", "L1_gnn_b_conv0", "L1_gnn_b_lin0", "L1_gnn_b_conv1", "L1_gnn_b_lin1"]


def kernel(**inputs):
    import numpy as np
    import concourse.bacc as bacc
    from concourse.bass_utils import run_bass_kernel_spmd

    arrays = {k: np.ascontiguousarray(inputs[k]) for k in _PLAIN}
    for k in ("W_conv0", "W_lin0", "W_conv1", "W_lin1"):
        arrays[k + "_T"] = np.ascontiguousarray(np.asarray(inputs["L1_gnn_" + k]).T)
    pad = GROUPS * GROUP * P - EDGES
    for k in ("src", "dst"):
        v = np.pad(np.asarray(inputs[k]), (0, pad), mode="edge")
        arrays[k] = np.ascontiguousarray(v.reshape(GROUPS * GROUP, P).T)
    v = np.pad(np.asarray(inputs["edge_attr_32"]), ((0, pad), (0, 0)), mode="edge")
    arrays["edge"] = np.ascontiguousarray(v.reshape(GROUPS, GROUP, P, E).transpose(1, 3, 0, 2).reshape(GROUP * E, GROUPS * P))

    nc = bacc.Bacc("TRN2", target_bir_lowering=False, num_devices=1)
    args, maps = {}, {}
    for k, v in arrays.items():
        maps["in_" + k] = v
        args[k] = nc.dram_tensor("in_" + k, v.shape, mybir.dt.from_np(v.dtype), kind="ExternalInput").ap()
    out = nc.dram_tensor("out_0", (NODES, D), F32, kind="ExternalOutput").ap()
    build(nc, args, out)
    r = run_bass_kernel_spmd(nc, [maps], core_ids=[0])
    return r.results[0]["out_0"]
```

```python
from contextlib import ExitStack

import concourse.bass as bass
from concourse import mybir

F32 = mybir.dt.float32
I32 = mybir.dt.int32
ALU = mybir.AluOpType
ACT = mybir.ActivationFunctionType
AX = mybir.AxisListType

P = 128
BANK = 512

NODES = 6250
EDGES = 100000
D = 128
E = 32
HID = 256
EPS = 1e-5

NODE_TILES = -(-NODES // P)
LAST_ROWS = NODES - (NODE_TILES - 1) * P
BATCH = BANK // D
BATCHES = -(-NODE_TILES // BATCH)
assert NODE_TILES - (BATCHES - 1) * BATCH == 1

GROUP = 4
TILES = -(-EDGES // P)
GROUPS = -(-TILES // GROUP)
LAST_EDGES = EDGES - (TILES - 1) * P
WINDOW = 80
WINDOWS = -(-NODES // WINDOW)
NODE_COLS = NODES + WINDOW
assert WINDOWS * WINDOW <= NODE_COLS and NODE_TILES * P <= NODE_COLS

SUPER = 4
LAG = SUPER + 1
AHEAD = 2
WIDE = LAG + AHEAD + 2
RING = 5
NODE_BUF = NODE_TILES * D
assert NODE_BUF + RING * GROUP * D <= WIDE * GROUP * HID
EDGE_CHUNK = 4
EDGE_CHUNKS = -(-GROUPS // EDGE_CHUNK)
ROUNDS = 3
NORM_LAG = 3
TABLE_SLOTS = (4, 1, 1)
COUNT, ONE = 0, 32


def tiles_of(g):
    return min(GROUP, TILES - g * GROUP)


def nodes_of(b):
    return min(BATCH, NODE_TILES - b * BATCH)


def edges_of(t):
    return P if t < TILES - 1 else LAST_EDGES


def stores_of(r):
    return [len(range(i, BATCHES, TABLE_SLOTS[r])) for i in range(TABLE_SLOTS[r])]


def beside(g, lag):
    b = g - 2 - lag
    return [b] if 0 <= b < BATCHES else []


def gathered():
    count, out = [0] * RING, []
    for n in range(ROUNDS * GROUPS):
        count[n % RING] += 16 * tiles_of(n % GROUPS)
        out.append(count[n % RING])
    return out


GATHERED = gathered()


def build(nc, a, out):
    with ExitStack() as ctx:
        def sb(name, shape, dt=F32):
            return ctx.enter_context(nc.sbuf_tensor(name, shape, dt))

        def ps(name, shape):
            return ctx.enter_context(nc.psum_tensor(name, shape, F32))

        def sem(name):
            return ctx.enter_context(nc.semaphore(name))

        table = [nc.dram_tensor("table_mlp", (NODES, HID), F32).ap(),
                 nc.dram_tensor("table_conv0", (NODES, D), F32).ap(),
                 nc.dram_tensor("table_conv1", (NODES, D), F32).ap()]

        x = sb("x", [P, NODE_BUF])
        hT = sb("hT", [P, NODE_TILES * P])
        acc = sb("acc", [P, 3, NODE_COLS])
        wide = sb("wide", [P, WIDE * GROUP * HID])
        hidden = wide[:, 0:NODE_BUF]
        ring = wide[:, NODE_BUF:NODE_BUF + RING * GROUP * D].rearrange("p (r q d) -> p r q d", r=RING, q=GROUP)
        act = [sb(f"act{i}", [P, GROUP * HID]) for i in range(2)]
        onehot = sb("onehot", [P, 2, GROUP, WINDOW])
        edge = sb("edge", [P, 2, EDGE_CHUNK * P])
        src_i = sb("src_i", [P, GROUPS * GROUP], I32)
        dst_f = sb("dst_f", [P, GROUPS * GROUP])
        dst_rel = sb("dst_rel", [P, GROUPS * GROUP])
        base_f = sb("base_f", [P, GROUPS])
        base_i = sb("base_i", [P, GROUPS], I32)
        span_i = sb("span_i", [P, 1], I32)
        window_lo = sb("window_lo", [P, 1])
        w1a = sb("w1a", [P, HID])
        w1b = sb("w1b", [P, GROUP, HID])
        b1 = sb("b1", [P, HID])
        wu = sb("wu", [P, 2, D])
        w2u = sb("w2u", [P, 2, D])
        bu2 = sb("bu2", [P, D])
        w_lin = [sb(f"w_lin{i}", [P, D]) for i in range(2)]
        w_conv = [sb(f"w_conv{i}", [P, D]) for i in range(2)]
        b_conv = sb("b_conv", [P, 2, D])
        g1 = sb("g1", [P, HID])
        be1 = sb("be1", [P, HID])
        gu = sb("gu", [P, D])
        beu = sb("beu", [P, D])
        ones = sb("ones", [P, P])
        ident = sb("ident", [P, P])
        iota = sb("iota", [P, WINDOW])
        centre = sb("centre", [P, 2, 9])
        sumsq = sb("sumsq", [P, 2, SUPER * GROUP])
        rstd = sb("rstd", [P, 2, SUPER * GROUP])
        newton = sb("newton", [P, SUPER * GROUP])
        guess = sb("guess", [P, SUPER * GROUP], I32)
        rcount = sb("rcount", [P, NODE_TILES])
        bn = sb("bn", [P, 2, BATCH, 6])
        mean_var = sb("mean_var", [P, 4, BATCH, 2])
        usq = sb("usq", [P, 2, BATCH])
        variance = sb("variance", [P, 2, 2 * BATCH])
        scale = sb("scale", [P, 4, 2 * BATCH])
        shift = sb("shift", [P, 4, BATCH])
        late = wide[:, 5 * GROUP * HID:]
        dst_i = late[:, 0:GROUPS * GROUP].bitcast(I32)
        lo_hi = late[:, 800:800 + 2 * GROUPS].rearrange("p (i g) -> p i g", i=2)
        span = late[:, 1200:1200 + GROUPS]
        span_max = late[:, 1396:1397]
        lo_hi_col = late[:, 1397:1401]
        iota_i = late[:, 1401:1401 + WINDOW].bitcast(I32)
        lo_hi_bc = late[:, 1500:1500 + 4 * P].rearrange("p (i c) -> p i c", i=4)
        b_parts = late[:, 2012:2012 + 4 * D].rearrange("p (i d) -> p i d", i=4)
        w2T = late[:, 2524:2524 + HID]
        b2 = late[:, 2780:2781]

        mm = ps("mm", [P, 4, BANK])
        seg = ps("seg", [P, 2, BANK])
        node = ps("node", [P, 2, BANK])

        s_w = sem("s_w")
        s_idx = sem("s_idx")
        s_x = [sem(f"s_x{i}") for i in range(BATCHES)]
        s_edge = [sem(f"s_edge{i}") for i in range(2)]
        s_rows = [sem(f"s_rows{i}") for i in range(RING)]
        s_table = [[sem(f"s_table{r}_{i}") for i in range(n)] for r, n in enumerate(TABLE_SLOTS)]
        s_out = sem("s_out")
        s_pad = sem("s_pad")
        s_const = sem("s_const")
        s_zero = sem("s_zero")
        s_weights = sem("s_weights")
        s_joint = sem("s_joint")
        s_jointc = sem("s_jointc")
        s_lohi = sem("s_lohi")
        s_lohiT = sem("s_lohiT")
        s_lohic = sem("s_lohic")
        s_base = sem("s_base")
        s_windows = sem("s_windows")
        link_v = sem("link_v")
        s_scale = [sem(f"s_scale{i}") for i in range(2)]
        s_h = [sem(f"s_h{i}") for i in range(2)]
        s_tr = [sem(f"s_tr{i}") for i in range(2)]
        s_hT = [sem(f"s_hT{i}") for i in range(2)]
        s_sum = [sem(f"s_sum{i}") for i in range(2)]
        s_p = sem("s_p")
        s_pc = sem("s_pc")
        s_u = sem("s_u")
        s_usq = sem("s_usq")
        s_un = sem("s_un")
        s_ub = sem("s_ub")
        s_ug = sem("s_ug")
        s_rezero = sem("s_rezero")
        s_cnt = sem("s_cnt")
        s_ew = sem("s_ew")
        s_copy = sem("s_copy")
        s_square = sem("s_square")
        s_scaled = sem("s_scaled")
        s_biased = sem("s_biased")
        s_gelu = sem("s_gelu")
        s_onehot = [sem(f"s_onehot{r}") for r in range(ROUNDS)]
        s_seg = [sem(f"s_seg{r}") for r in range(ROUNDS)]
        s_flush = [sem(f"s_flush{r}") for r in range(ROUNDS)]
        g_hot = sem("g_hot")
        g_seg = sem("g_seg")
        s_own = [sem(f"s_own{i}") for i in range(2)]
        s_ownc = [sem(f"s_ownc{i}") for i in range(2)]
        s_conv = [sem(f"s_conv{i}") for i in range(2)]
        s_res = [sem(f"s_res{i}") for i in range(2)]
        s_hid = sem("s_hid")
        s_hidT = sem("s_hidT")
        s_hidTc = sem("s_hidTc")

        def table_rows(t, b):
            r0 = b * BATCH * P
            if b == BATCHES - 1:
                return t[r0:NODES, :]
            return t[r0:r0 + BATCH * P, :].rearrange("(t p) d -> p t d", p=P)

        def stored(v, b):
            return v[0:LAST_ROWS, :] if b == BATCHES - 1 else v.rearrange("p (t d) -> p t d", t=BATCH)

        def batch(t, b):
            return t[:, b * BANK:b * BANK + nodes_of(b) * D]

        def tile(t, j):
            return t[:, j * P:(j + 1) * P]

        def tiles(v, n):
            return v.rearrange("p (t d) -> p t d", t=n)

        def mlp_buf(g):
            i = g % WIDE * GROUP * HID
            return wide[:, i:i + GROUP * HID]

        def phase0_h(b):
            i = b // 2 % 2 * BANK
            return act[b % 2][:, i:i + nodes_of(b) * D]

        def row(name):
            return a[name].rearrange("(a n) -> a n", a=1)

        weight_loads = [(w1a[:, :], a["L0_gnn_W1"][0:D, :])]
        weight_loads += [(w1b[E * q:E * q + E, q, :], a["L0_gnn_W1"][D:D + E, :]) for q in range(GROUP)]
        weight_loads += [(v[:, :], a["L0_gnn_" + k].partition_broadcast(P))
                         for v, k in ((b1, "b1"), (g1, "g1"), (be1, "be1"), (gu, "gu"), (beu, "beu"))]
        weight_loads += [(wu[:, :, :], a["L0_gnn_Wu"].rearrange("(h p) n -> p h n", p=P)), (bu2[ONE:ONE + 1, :], row("L0_gnn_bu")),
                         (w2T, a["L0_gnn_W2_T"]), (b2, a["L0_gnn_b2"].rearrange("(p a) -> p a", a=1))]
        weight_loads += [(w[i][:, :], a[f"L1_gnn_W_{k}{i}_T"]) for k, w in (("lin", w_lin), ("conv", w_conv)) for i in range(2)]
        weight_loads += [(b_parts[:, i, :], a["L1_gnn_b_" + k].partition_broadcast(P))
                         for i, k in enumerate(("conv0", "lin0", "conv1", "lin1"))]

        block = ctx.enter_context(nc.Block())

        @block.sync
        def _(sp):
            def load_x(b):
                v = batch(x, b)
                sp.dma_start(v[0:LAST_ROWS, :] if b == BATCHES - 1 else tiles(v, BATCH), table_rows(a["x"], b))\
                  .then_inc(s_x[b], 16)

            load_x(0)
            load_x(1)
            sp.wait_ge(s_pad, 3)
            for v, w in weight_loads:
                sp.dma_start(v, w).then_inc(s_w, 16)
            for b in range(2, BATCHES):
                load_x(b)
            sp.dma_start(dst_i, a["dst"]).then_inc(s_idx, 16)
            sp.dma_start(src_i[:, :], a["src"]).then_inc(s_idx, 16)

            def load_edges(c):
                if c >= 2:
                    sp.wait_ge(s_ew, EDGE_CHUNK * (c - 1))
                sp.dma_start(edge[:, c % 2, :], a["edge"][:, c * EDGE_CHUNK * P:(c + 1) * EDGE_CHUNK * P])\
                  .then_inc(s_edge[c % 2], 16)

            load_edges(0)
            load_edges(1)
            for b in range(BATCHES):
                sp.wait_ge(s_pc, b + 1)
                v = wide[:, b % 4 * GROUP * HID:(b % 4 * GROUP + nodes_of(b)) * HID]
                sp.dma_start(table_rows(table[0], b), stored(v, b)).then_inc(s_table[0][b % 4], 16)
            for c in range(2, EDGE_CHUNKS):
                load_edges(c)
            for b in range(BATCHES):
                sp.wait_ge(s_h[1], b + 1)
                sp.dma_start(table_rows(table[1], b), stored(batch(hidden, b), b)).then_inc(s_table[1][0], 16)
            for b in range(BATCHES):
                sp.wait_ge(s_hid, b + 1)
                sp.dma_start(table_rows(table[2], b), stored(batch(hidden, b), b)).then_inc(s_table[2][0], 16)
            for b in range(BATCHES):
                sp.wait_ge(s_res[1], b + 1)
                sp.dma_start(table_rows(out, b), stored(batch(x, b), b)).then_inc(s_out, 16)
            sp.wait_ge(s_out, 16 * BATCHES)

        @block.gpsimd
        def _(pool):
            pool.memset(w1b[:, :, :], 0.0).then_inc(s_pad, 1)
            pool.memset(bu2[:, :], 0.0).then_inc(s_pad, 1)
            pool.memset(tile(x, NODE_TILES - 1), 0.0).then_inc(s_pad, 1)
            pool.memset(ident[:, :], 0.0).then_inc(s_const, 1)
            pool.memset(ones[:, :], 1.0).then_inc(s_const, 1)
            pool.iota(iota_i, pattern=[[1, WINDOW]], base=0, channel_multiplier=0).then_inc(s_const, 1)
            pool.wait_ge(s_const, 3)
            pool.affine_select(out=ident[:, :], in_=ident[:, :], compare_op=ALU.not_equal, fill=1.0,
                               base=0, pattern=[[-1, P]], channel_multiplier=1).then_inc(s_const, 1)
            pool.memset(ones[:, ONE:ONE + 1], 0.0).then_inc(s_const, 1)
            pool.memset(acc[:, :, :], 0.0).then_inc(s_zero, 1)
            pool.wait_ge(s_zero, 1)
            pool.memset(acc[ONE:ONE + 1, 2, :], 1.0).then_inc(s_zero, 1)
            pool.wait_ge(s_zero, 2)

            def add_to_x(phase, b, done):
                pool.wait_ge(done, b + 1)
                v = phase0_h(b) if phase == 0 else act[b % 2][:, 0:nodes_of(b) * D]
                pool.tensor_tensor(batch(x, b), batch(x, b), v, ALU.add).then_inc(s_sum[phase], 1)

            for b in range(BATCHES):
                add_to_x(0, b, s_h[0])
            pool.wait_ge(s_idx, 32)
            for r in range(ROUNDS):
                if r == 1:
                    for b in range(BATCHES):
                        pool.wait_ge(s_u, b + 1)
                        to = NODE_COLS if b == BATCHES - 1 else (b + 1) * BANK
                        pool.memset(acc[:, 0:2, b * BANK:to], 0.0).then_inc(s_rezero, 1)
                        add_to_x(1, b, s_ug)
                for s, n in zip(s_table[r], stores_of(r)):
                    pool.wait_ge(s, 16 * n)
                for g in range(GROUPS):
                    n = r * GROUPS + g
                    if r == 0:
                        pool.wait_ge(s_copy, g + 1)
                    elif g >= RING:
                        pool.wait_ge(s_seg[r], g - RING + 1)
                    for q in range(tiles_of(g)):
                        t = g * GROUP + q
                        index = bass.IndirectOffsetOnAxis(ap=src_i[:, t:t + 1], axis=0)
                        if r == 0:
                            ins = pool.indirect_dma_start(mlp_buf(g)[:, q * HID:(q + 1) * HID], None, table[r], index,
                                                          compute_op=ALU.add)
                        else:
                            ins = pool.indirect_dma_start(ring[:, n % RING, q, :], None, table[r], index)
                        ins.then_inc(s_rows[n % RING], 16)

        @block.tensor
        def _(pe):
            def transposes(phase, b):
                pe.wait_ge(s_h[phase], b + 1)
                if b >= 2:
                    pe.wait_ge(s_hT[phase], b - 1)
                v = phase0_h(b) if phase == 0 else batch(hidden, b)
                for j in range(nodes_of(b)):
                    last = pe.transpose(seg[:, b % 2, j * P:(j + 1) * P], tile(v, j), ident[:, :])
                last.then_inc(s_tr[phase], 1)

            def mlp_table(b):
                pe.wait_ge(s_hT[0], b + 1)
                if b >= 2:
                    pe.wait_ge(s_pc, b - 1)
                for j in range(nodes_of(b)):
                    last = pe.matmul(mm[:, 2 * (b % 2) + j // 2, (j % 2) * HID:(j % 2 + 1) * HID],
                                     tile(hT, b * BATCH + j), w1a[:, :], start=True, stop=True)
                last.then_inc(s_p, 1)

            def edge_part(g):
                c = g // EDGE_CHUNK
                pe.wait_ge(s_edge[c % 2], 16 * (c // 2 + 1))
                if g >= 2:
                    pe.wait_ge(s_copy, g - 1)
                col = (g % EDGE_CHUNK) * P
                for q in range(tiles_of(g)):
                    last = pe.matmul(mm[:, 2 * (g % 2) + q // 2, (q % 2) * HID:(q % 2 + 1) * HID],
                                     edge[:, c % 2, col:col + P], w1b[:, q, :], start=True, stop=True)
                last.then_inc(s_ew, 1)

            pe.wait_ge(s_const, 4)
            for b in range(BATCHES + 1):
                if b < BATCHES:
                    transposes(0, b)
                if b == 1:
                    pe.wait_ge(s_weights, 1)
                if b >= 1:
                    mlp_table(b - 1)
            for h in range(2):
                pe.matmul(node[:, 0, h * D:(h + 1) * D], w2T[:, h * D:(h + 1) * D], wu[:, 1, :], start=True, stop=True)
            pe.matmul(node[0:1, 0, 2 * D:3 * D], b2, wu[:, 1, :], start=True, stop=True).then_inc(s_joint, 1)
            pe.wait_ge(s_pc, BATCHES)
            edge_part(0)
            edge_part(1)

            half = GROUPS // 2
            pe.wait_ge(s_lohi, 1)
            for i in range(4):
                last = pe.transpose(node[0:half, 1, i * P:(i + 1) * P],
                                    lo_hi[:, i // 2, (i % 2) * half:(i % 2 + 1) * half], ident[:, :])
            last.then_inc(s_lohiT, 1)
            pe.wait_ge(s_lohic, 1)
            for i in range(4):
                last = pe.matmul(node[:, 0, i * half:(i + 1) * half], lo_hi_bc[0:half, i, :],
                                 ident[0:half, 0:half], start=True, stop=True)
            last.then_inc(s_base, 1)

            def window_sums(r, g):
                n, nt = r * GROUPS + g, tiles_of(g)
                for h in ([2, 0, 1] if r == 0 else [0]):
                    for q in range(nt):
                        k = edges_of(g * GROUP + q)
                        if h == 2:
                            v = ones[0:k, :]
                        elif r == 0:
                            v = act[g % 2][0:k, q * HID + h * D:q * HID + (h + 1) * D]
                        else:
                            v = ring[0:k, n % RING, q, :]
                        last = pe.matmul(seg[:, g % 2, h * WINDOW:(h + 1) * WINDOW], v,
                                         onehot[0:k, g % 2, q, :], start=(q == 0), stop=(q == nt - 1))
                return last

            def segment(r, g, general):
                n = r * GROUPS + g
                if g >= 2:
                    pe.wait_ge(s_flush[r], g - 1)
                if r == 0:
                    pe.wait_ge(s_gelu, g + 1)
                else:
                    pe.wait_ge(s_rows[n % RING], GATHERED[n])
                if not general:
                    pe.wait_ge(s_onehot[r], g + 1)
                    window_sums(r, g).then_inc(s_seg[r], 1)
                    return
                with pe.Fori(0, WINDOWS):
                    pe.wait_ge(g_hot, 1)
                    pe.sem_clear(g_hot)
                    window_sums(r, g).then_inc(g_seg, 1)
                pe.drain().then_inc(s_seg[r], 1)

            def update(b):
                if b >= 4:
                    pe.wait_ge(s_un, b - 3)
                for j in range(nodes_of(b)):
                    o, t = mm[:, b % 4, j * D:(j + 1) * D], b * BATCH + j
                    pe.matmul(o, tile(hT, t), wu[:, 0, :], start=True, stop=False)
                    pe.matmul(o, tile(acc[:, 0, :], t), w2u[:, 0, :], start=False, stop=False)
                    pe.matmul(o, tile(acc[:, 1, :], t), w2u[:, 1, :], start=False, stop=False)
                    last = pe.matmul(o, tile(acc[:, 2, :], t), bu2[:, :], start=False, stop=True)
                last.then_inc(s_u, 1)

            def node_products(bank, b, lhs, rhs, done):
                for j in range(nodes_of(b)):
                    last = pe.matmul(mm[:, bank, j * D:(j + 1) * D], tile(lhs, b * BATCH + j), rhs, start=True, stop=True)
                last.then_inc(done, 1)

            def own_part(i, b):
                if i == 0:
                    if b >= 4:
                        pe.wait_ge(s_ownc[0], b - 3)
                    node_products(b % 4, b, hT, w_lin[0][:, :], s_own[0])
                else:
                    pe.wait_ge(s_hidTc, b + 1)
                    if b >= 2:
                        pe.wait_ge(s_ownc[1], b - 1)
                    node_products(2 + b % 2, b, hT, w_lin[1][:, :], s_own[1])

            def hidden_transposes(b):
                if b == 0:
                    pe.wait_ge(s_hid, BATCHES)
                if b >= 2:
                    pe.wait_ge(s_hidTc, b - 1)
                for j in range(nodes_of(b)):
                    last = pe.transpose(mm[:, b % 2, j * P:(j + 1) * P], tile(hidden, b * BATCH + j), ident[:, :])
                last.then_inc(s_hidT, 1)

            def mean_parts(i):
                pe.wait_ge(s_flush[i + 1], GROUPS)
                pe.wait_ge(s_ownc[i], BATCHES)
                for b in range(BATCHES):
                    if b >= 4:
                        pe.wait_ge(s_res[i], b - 3)
                    node_products(b % 4, b, acc[:, i, :], w_conv[i][:, :], s_conv[i])

            def rounds(general):
                for i in range(AHEAD, GROUPS + LAG + 1 + AHEAD):
                    if i < GROUPS:
                        edge_part(i)
                    if i - AHEAD > LAG:
                        segment(0, i - AHEAD - LAG - 1, general)
                pe.wait_ge(s_flush[0], GROUPS)
                pe.wait_ge(s_jointc, 1)
                for b in range(BATCHES + 6):
                    if b < BATCHES:
                        update(b)
                    if b >= 6:
                        transposes(1, b - 6)
                for j in range(NODE_TILES):
                    last = pe.matmul(node[:, 0, j:j + 1], tile(acc[:, 2, :], j), ident[:, COUNT:COUNT + 1], start=True, stop=True)
                last.then_inc(s_cnt, 1)
                pe.wait_ge(s_hT[1], BATCHES)
                for g in range(GROUPS):
                    segment(1, g, general)
                    for b in beside(g, 0):
                        own_part(0, b)
                mean_parts(0)
                for g in range(GROUPS):
                    segment(2, g, general)
                    for b in beside(g, 0):
                        hidden_transposes(b)
                    for b in beside(g, 1):
                        own_part(1, b)
                mean_parts(1)

            pe.wait_ge(s_windows, 1)
            widest = pe.value_load(span_i[0:1, 0:1], min_val=0, max_val=NODES)
            with pe.If(widest >= WINDOW):
                rounds(True)
            with pe.Else():
                rounds(False)

        @block.scalar
        def _(ac):
            def relu_norm(phase, b):
                ac.wait_ge(s_scale[phase], b + 1)
                if phase == 0 and b >= 4:
                    ac.wait_ge(s_tr[0], b - 3)
                    ac.wait_ge(s_sum[0], b - 3)
                o = phase0_h(b) if phase == 0 else batch(hidden, b)
                first = 0 if phase == 0 else BATCH
                slot = (b if phase == 0 else b + NORM_LAG) % 4
                for j in range(nodes_of(b)):
                    last = ac.activation(tile(o, j), tile(x, b * BATCH + j), ACT.Relu, bias=shift[:, slot, j:j + 1],
                                         scale=scale[:, slot, first + j:first + j + 1])
                last.then_inc(s_h[phase], 1)

            def copy_hT(phase, b):
                ac.wait_ge(s_tr[phase], b + 1)
                ac.activation(batch(hT, b), seg[:, b % 2, 0:nodes_of(b) * P], ACT.Copy).then_inc(s_hT[phase], 1)

            for b in range(BATCHES + 1):
                if b < BATCHES:
                    relu_norm(0, b)
                if b >= 1:
                    copy_hT(0, b - 1)

            def copy_edge_part(g):
                k = tiles_of(g) * HID
                ac.wait_ge(s_ew, g + 1)
                if g == 0:
                    for s, n in zip(s_table[0], stores_of(0)):
                        ac.wait_ge(s, 16 * n)
                if g == 5:
                    ac.wait_ge(s_windows, 1)
                if g >= WIDE:
                    ac.wait_ge(s_gelu, g - WIDE + 1)
                ac.activation(mlp_buf(g)[:, 0:k], mm[:, :, :].rearrange("p b c -> p (b c)")[:, (g % 2) * 2 * BANK:(g % 2) * 2 * BANK + k],
                              ACT.Copy).then_inc(s_copy, 1)

            def squares(g):
                ac.wait_ge(s_rows[g % RING], GATHERED[g])
                if g >= 1:
                    ac.wait_ge(s_square, g)
                if g % SUPER == 0 and g >= 2 * SUPER:
                    ac.wait_ge(s_scaled, g - 2 * SUPER + 1)
                for q in range(tiles_of(g)):
                    t = (g % SUPER) * GROUP + q
                    last = ac.activation(node[:, q // 2, (q % 2) * HID:(q % 2 + 1) * HID], mlp_buf(g)[:, q * HID:(q + 1) * HID],
                                         ACT.Square, accum_out=sumsq[:, g // SUPER % 2, t:t + 1])
                last.then_inc(s_square, 1)

            def gelu(g):
                k = tiles_of(g) * HID
                ac.wait_ge(s_biased, g + 1)
                if g >= 2:
                    ac.wait_ge(s_seg[0], g - 1)
                ac.activation(act[g % 2][:, 0:k], mlp_buf(g)[:, 0:k], ACT.Gelu).then_inc(s_gelu, 1)

            ac.wait_ge(s_sum[0], BATCHES)
            copy_edge_part(0)
            copy_edge_part(1)
            for g in range(GROUPS + LAG):
                if g + AHEAD < GROUPS:
                    copy_edge_part(g + AHEAD)
                if g < GROUPS:
                    squares(g)
                if g >= LAG:
                    gelu(g - LAG)

            ac.wait_ge(s_seg[0], GROUPS)
            for i in range(BATCHES + NORM_LAG + 2):
                if i < BATCHES:
                    ac.wait_ge(s_u, i + 1)
                    if i >= 1:
                        ac.wait_ge(s_usq, i)
                    if i >= 2:
                        ac.wait_ge(s_un, i - 1)
                    for j in range(nodes_of(i)):
                        last = ac.activation(act[0][:, (4 + j) * D:(5 + j) * D], mm[:, i % 4, j * D:(j + 1) * D], ACT.Square,
                                             accum_out=usq[:, i % 2, j:j + 1])
                    last.then_inc(s_usq, 1)
                b = i - 2
                if 0 <= b < BATCHES:
                    v = act[b % 2][:, 0:nodes_of(b) * D]
                    ac.wait_ge(s_ub, b + 1)
                    ac.activation(v, v, ACT.Gelu).then_inc(s_ug, 1)
                if 0 <= i - NORM_LAG - 1 < BATCHES:
                    relu_norm(1, i - NORM_LAG - 1)
                if 0 <= i - NORM_LAG - 2 < BATCHES:
                    copy_hT(1, i - NORM_LAG - 2)

            for b in range(BATCHES):
                ac.wait_ge(s_res[0], b + 1)
                ac.activation(batch(hidden, b), batch(hidden, b), ACT.Relu).then_inc(s_hid, 1)
            for b in range(BATCHES):
                ac.wait_ge(s_hidT, b + 1)
                ac.activation(batch(hT, b), mm[:, b % 2, 0:nodes_of(b) * P], ACT.Copy).then_inc(s_hidTc, 1)

        @block.vector
        def _(ve):
            linked = [0]

            def link(ins):
                linked[0] += 1
                ins.then_inc(link_v, 1)
                ve.wait_ge(link_v, linked[0])

            def tt(o, i0, i1, op):
                return ve.tensor_tensor(o, i0, i1, op)

            def ts(o, i0, s1, s2, op0, op1=None):
                if op1 is None:
                    return ve.tensor_scalar(o, i0, s1, None, op0)
                return ve.tensor_scalar(o, i0, s1, s2, op0, op1)

            def stt(o, i0, s, i1, op0, op1):
                return ve.scalar_tensor_tensor(out=o, in0=i0, scalar=s, in1=i1, op0=op0, op1=op1)

            class Chain:

                def __init__(self):
                    self.steps, self.result = [], 0

                def add(self, make):
                    def step():
                        self.wait()
                        linked[0] += 1
                        make().then_inc(link_v, 1)
                        self.result = linked[0]
                    self.steps.append(step)

                def wait(self):
                    if self.result:
                        ve.wait_ge(link_v, self.result)

            def weave(chain, others):
                others = list(others)
                for s in chain.steps:
                    s()
                    if others:
                        others.pop(0)()
                for o in others:
                    o()
                chain.wait()

            def inverse_root(chain, y, v):
                n = v.shape[1]
                gi, t = guess[:, 0:n], newton[:, 0:n]
                chain.add(lambda: ts(gi, v.bitcast(I32), 1, None, ALU.logical_shift_right))
                chain.add(lambda: ts(gi, gi, -1.0, float(0x5F3759DF), ALU.mult, ALU.add))
                for g in (gi.bitcast(F32), y, y):
                    chain.add(lambda g=g: tt(t, g, g, ALU.mult))
                    chain.add(lambda g=g: stt(t, t, -0.5, v, ALU.mult, ALU.mult))
                    chain.add(lambda g=g: stt(y, t, 1.5, g, ALU.add, ALU.mult))

            def statistics(b):
                slot = b % 2
                out = []
                for j in range(nodes_of(b)):
                    out.append(lambda j=j: ve.bn_stats(bn[:, slot, j, :], tile(x, b * BATCH + j)))
                def aggregate():
                    for j in range(nodes_of(b)):
                        ins = ve.bn_aggr(mean_var[:, b % 4, j, :], bn[:, slot, j, :])
                    link(ins)
                def flushed():
                    linked[0] += 1
                    ve.bn_stats(bn[:, slot, nodes_of(b) - 1, :], tile(x, b * BATCH + nodes_of(b) - 1)).then_inc(link_v, 1)
                    ve.wait_ge(link_v, linked[0])
                out[-1] = flushed
                out.append(aggregate)
                return out

            def norm_shift(b, slot, first):
                n = nodes_of(b)
                return stt(shift[:, slot, 0:n], mean_var[:, b % 4, 0:n, 0], -1.0, scale[:, slot, first:first + n],
                           ALU.mult, ALU.mult)

            def weights():
                ve.wait_ge(s_w, 16 * len(weight_loads))
                for o, w in ((slice(0, 1), w1a[:, :]), (slice(1, 5), w1b[:, :, :]), (slice(5, 6), b1[:, :]),
                             (slice(6, 8), wu[:, :, :]), (slice(8, 9), bu2[:, :])):
                    last = ve.tensor_reduce(centre[:, 0, o], w, AX.X, ALU.add)
                link(last)
                ts(centre[:, 1, 0:6], centre[:, 0, 0:6], -1.0 / HID, None, ALU.mult)
                link(ts(centre[:, 1, 6:9], centre[:, 0, 6:9], -1.0 / D, None, ALU.mult))
                for k, w in ([(0, w1a[:, :]), (5, b1[:, :]), (6, wu[:, 0, :]), (7, wu[:, 1, :]), (8, bu2[:, :])]
                             + [(1 + q, w1b[:, q, :]) for q in range(GROUP)]):
                    last = ts(w, w, centre[:, 1, k:k + 1], None, ALU.add)
                last = ts(g1[:, :], g1[:, :], float(HID) ** 0.5, None, ALU.mult)
                last.then_inc(s_weights, 1)
                ve.wait_ge(s_weights, 1)

            def table_copy(b):
                out = []
                n = nodes_of(b)
                def one(i):
                    if i == 0:
                        ve.wait_ge(s_p, b + 1)
                        if b >= 4:
                            ve.wait_ge(s_table[0][b % 4], 16 * (b // 4))
                    k = min(2, n - i)
                    o = tiles(wide[:, (b % 4 * GROUP + i) * HID:(b % 4 * GROUP + i + k) * HID], k)
                    ins = tt(o, tiles(mm[:, 2 * (b % 2) + i // 2, 0:k * HID], k),
                             b1[:, :].unsqueeze(1).to_broadcast([P, k, HID]), ALU.add)
                    if i + k == n:
                        ins.then_inc(s_pc, 1)
                return [lambda i=i: one(i) for i in range(0, n, 2)]

            for b in range(BATCHES + 3):
                chain, others = Chain(), []
                if b < BATCHES:
                    n = nodes_of(b)
                    if b == 0:
                        ve.wait_ge(s_x[0], 16)
                        for s in statistics(0):
                            s()
                    v = variance[:, b % 2, 0:n]
                    chain.add(lambda: ts(v, mean_var[:, b % 4, 0:n, 1], EPS, None, ALU.add))
                    if b >= 4:
                        ve.wait_ge(s_h[0], b - 3)
                    inverse_root(chain, scale[:, b % 4, 0:n], v)
                if b + 1 < BATCHES:
                    ve.wait_ge(s_x[b + 1], 16)
                    others += statistics(b + 1)
                if b >= 3:
                    if b == 3:
                        weights()
                    others += table_copy(b - 3)
                weave(chain, others)
                if b < BATCHES:
                    norm_shift(b, b % 4, 0).then_inc(s_scale[0], 1)

            ve.wait_ge(s_idx, 32)
            link(ve.tensor_copy(dst_f[:, :], dst_i))
            by_group = dst_f[:, :].rearrange("p (g q) -> p g q", q=GROUP)
            ve.tensor_reduce(lo_hi[:, 0, :], by_group, AX.X, ALU.min)
            ve.tensor_reduce(lo_hi[:, 1, :], by_group, AX.X, ALU.max).then_inc(s_lohi, 1)
            for i in range(2):
                tt(b_conv[:, i, :], b_parts[:, 2 * i, :], b_parts[:, 2 * i + 1, :], ALU.add)
            ve.wait_ge(s_joint, 1)
            ve.tensor_copy(w2u[:, :, :], tiles(node[:, 0, 0:2 * D], 2))
            ve.tensor_copy(bu2[COUNT:COUNT + 1, :], node[COUNT:COUNT + 1, 0, 2 * D:3 * D]).then_inc(s_jointc, 1)
            ve.wait_ge(s_lohiT, 1)
            half = GROUPS // 2
            v = node[0:half, 1, :].rearrange("p (i c) -> p i c", i=4)
            ve.tensor_reduce(lo_hi_col[0:half, 0:2], v[:, 0:2, :], AX.X, ALU.min)
            link(ve.tensor_reduce(lo_hi_col[0:half, 2:4], v[:, 2:4, :], AX.X, ALU.max))
            ve.tensor_copy(lo_hi_bc[0:half, :, :], lo_hi_col[0:half, :].unsqueeze(2).to_broadcast([half, 4, P]))\
              .then_inc(s_lohic, 1)
            ve.wait_ge(s_base, 1)
            link(ve.tensor_copy(base_f[:, :], node[:, 0, 0:GROUPS]))
            ve.tensor_copy(base_i[:, :], base_f[:, :])
            link(tt(span, node[:, 0, GROUPS:2 * GROUPS], base_f[:, :], ALU.subtract))
            link(ve.tensor_reduce(span_max, span, AX.X, ALU.max))
            ve.tensor_copy(span_i[:, :], span_max)
            ve.wait_ge(s_const, 5)
            ve.tensor_copy(iota[:, :], iota_i)
            tt(dst_rel[:, :].rearrange("p (g q) -> p g q", q=GROUP), by_group,
               base_f[:, :].unsqueeze(2).to_broadcast([P, GROUPS, GROUP]), ALU.subtract).then_inc(s_windows, 1)
            ve.wait_ge(s_windows, 1)

            def hot(r, g, general):
                if general:
                    return
                if g >= 2:
                    ve.wait_ge(s_seg[r], g - 1)
                n, t = tiles_of(g), g * GROUP
                tt(onehot[:, g % 2, 0:n, :], iota[:, :].unsqueeze(1).to_broadcast([P, n, WINDOW]),
                   dst_rel[:, t:t + n].unsqueeze(2).to_broadcast([P, n, WINDOW]), ALU.is_equal).then_inc(s_onehot[r], 1)

            def add_window(r, g, start):
                parts = slice(0, 3) if r == 0 else slice(r - 1, r)
                n = 3 if r == 0 else 1
                o = acc[:, parts, bass.ds(start, WINDOW)]
                return tt(o, o, seg[:, g % 2, 0:n * WINDOW].rearrange("p (h w) -> p h w", h=n), ALU.add)

            def flush(r, g, general):
                if not general:
                    start = ve.value_load(base_i[0:1, g:g + 1], min_val=0, max_val=NODES - 1)
                    ve.wait_ge(s_seg[r], g + 1)
                    if g >= 1:
                        ve.wait_ge(s_flush[r], g)
                    add_window(r, g, start).then_inc(s_flush[r], 1)
                    return
                ve.memset(window_lo[:, :], 0.0)
                with ve.Fori(0, WINDOWS) as w:
                    ve.drain()
                    for q in range(tiles_of(g)):
                        t = g * GROUP + q
                        last = ts(onehot[:, g % 2, q, :], iota[:, :], window_lo[:, 0:1], dst_f[:, t:t + 1],
                                  ALU.add, ALU.is_equal)
                    last.then_inc(g_hot, 1)
                    ve.wait_ge(g_seg, 1)
                    ve.sem_clear(g_seg)
                    add_window(r, g, w * WINDOW)
                    ts(window_lo[:, :], window_lo[:, :], float(WINDOW), None, ALU.add)
                ve.drain().then_inc(s_flush[r], 1)

            def mlp_round(general):
                inverted = {}

                def invert(i):
                    first = i * SUPER
                    last = min(first + SUPER, GROUPS) - 1
                    n = (last - first) * GROUP + tiles_of(last)
                    v = sumsq[:, i % 2, 0:n]
                    chain = inverted[i] = Chain()

                    def begin():
                        ve.wait_ge(s_square, last + 1)
                        return ts(v, v, HID * EPS, None, ALU.add)

                    chain.add(begin)
                    inverse_root(chain, rstd[:, i % 2, 0:n], v)
                    return chain

                def normalise(g):
                    k = tiles_of(g)

                    def scaled(q):
                        if q == 0:
                            inverted[g // SUPER].wait()
                        v, t = mlp_buf(g)[:, q * HID:(q + 1) * HID], (g % SUPER) * GROUP + q
                        ins = stt(v, v, rstd[:, g // SUPER % 2, t:t + 1], g1[:, :], ALU.mult, ALU.mult)
                        if q == k - 1:
                            ins.then_inc(s_scaled, 1)

                    def biased():
                        ve.wait_ge(s_scaled, g + 1)
                        v = tiles(mlp_buf(g)[:, 0:k * HID], k)
                        tt(v, v, be1[:, :].unsqueeze(1).to_broadcast([P, k, HID]), ALU.add).then_inc(s_biased, 1)

                    return [lambda q=q: scaled(q) for q in range(k)], biased

                for i in range(GROUPS + LAG + 1):
                    others, g = [], i - LAG
                    if 0 <= g < GROUPS:
                        scaled, biased = normalise(g)
                        others = scaled + [lambda: hot(0, g, general), biased]
                    if g >= 1:
                        others.append(lambda: flush(0, g - 1, general))
                    if i % SUPER == 0 and 0 < i <= GROUPS:
                        first = others.pop(0) if others else lambda: None
                        first()
                        weave(invert(i // SUPER - 1), others)
                    else:
                        for o in others:
                            o()

            def node_update():
                inverted = {}

                def normalise_u(b):
                    n = nodes_of(b)
                    v = act[b % 2][:, 0:n * D]

                    def scaled(j):
                        if j == 0 and b >= 2:
                            ve.wait_ge(s_sum[1], b - 1)
                        ins = stt(tile(v, j), mm[:, b % 4, j * D:(j + 1) * D], scale[:, b % 4, j:j + 1], gu[:, :], ALU.mult, ALU.mult)
                        if j == n - 1:
                            ins.then_inc(s_un, 1)

                    def biased():
                        ve.wait_ge(s_un, b + 1)
                        tt(tiles(v, n), tiles(v, n), beu[:, :].unsqueeze(1).to_broadcast([P, n, D]), ALU.add).then_inc(s_ub, 1)

                    return [lambda j=j: scaled(j) for j in range(n)] + [biased]

                link(ve.memset(variance[:, :, :], 1.0))
                for i in range(BATCHES + NORM_LAG):
                    others = normalise_u(i - 1) if 1 <= i <= BATCHES else []
                    b = i - NORM_LAG
                    chain = Chain()
                    v = variance[:, i % 2, :]
                    if b >= 0:
                        ve.wait_ge(s_sum[1], b + 1)
                        for s in statistics(b):
                            s()
                        chain.add(lambda: ts(v[:, BATCH:BATCH + nodes_of(b)], mean_var[:, b % 4, 0:nodes_of(b), 1], EPS, None, ALU.add))
                    if i < BATCHES:
                        ve.wait_ge(s_usq, i + 1)
                        chain.add(lambda: ts(v[:, 0:nodes_of(i)], usq[:, i % 2, 0:nodes_of(i)], 1.0 / D, EPS, ALU.mult, ALU.add))
                    if b >= 4:
                        ve.wait_ge(s_h[1], b - 3)
                    inverse_root(chain, scale[:, i % 4, :], v)
                    weave(chain, others)
                    if b >= 0:
                        norm_shift(b, i % 4, BATCH).then_inc(s_scale[1], 1)

            def own_copy(i, b):
                n = nodes_of(b)
                ve.wait_ge(s_own[i], b + 1)
                bias = b_conv[:, i, :].unsqueeze(1).to_broadcast([P, n, D])
                if i == 0:
                    if b == 0:
                        for s, k in zip(s_table[1], stores_of(1)):
                            ve.wait_ge(s, 16 * k)
                    tt(tiles(batch(hidden, b), n), tiles(mm[:, b % 4, 0:n * D], n), bias, ALU.add).then_inc(s_ownc[0], 1)
                else:
                    v = batch(x, b)
                    link(tt(v, v, mm[:, 2 + b % 2, 0:n * D], ALU.add))
                    tt(tiles(v, n), tiles(v, n), bias, ALU.add).then_inc(s_ownc[1], 1)

            def conv_round(r, general):
                if r == 1:
                    ve.wait_ge(s_rezero, BATCHES)
                for g in range(GROUPS + 1):
                    if g < GROUPS:
                        hot(r, g, general)
                    if g >= 1:
                        flush(r, g - 1, general)
                        for b in beside(g - 1, r - 1):
                            own_copy(r - 1, b)
                    if r == 1 and g == 1:
                        ve.wait_ge(s_cnt, 1)
                        link(ts(rcount[:, :], node[:, 0, 0:NODE_TILES], 1.0, None, ALU.max))
                        link(ve.reciprocal(rcount[:, :], rcount[:, :]))

            def add_means(i):
                v = hidden if i == 0 else x
                ve.wait_ge(s_ownc[i], BATCHES)
                for b in range(BATCHES):
                    ve.wait_ge(s_conv[i], b + 1)
                    for j in range(nodes_of(b)):
                        t = b * BATCH + j
                        last = stt(tile(v, t), mm[:, b % 4, j * D:(j + 1) * D], rcount[:, t:t + 1], tile(v, t), ALU.mult, ALU.add)
                    last.then_inc(s_res[i], 1)

            def rounds(general):
                mlp_round(general)
                node_update()
                conv_round(1, general)
                add_means(0)
                conv_round(2, general)
                add_means(1)

            ve.wait_ge(s_zero, 2)
            widest = ve.value_load(span_i[0:1, 0:1], min_val=0, max_val=NODES)
            before = linked[0]
            with ve.If(widest >= WINDOW):
                rounds(True)
            linked[0] = before
            with ve.Else():
                rounds(False)


_PLAIN = ["x", "L0_gnn_W1", "L0_gnn_b1", "L0_gnn_g1", "L0_gnn_be1", "L0_gnn_b2", "L0_gnn_Wu", "L0_gnn_bu",
          "L0_gnn_gu", "L0_gnn_beu", "L1_gnn_b_conv0", "L1_gnn_b_lin0", "L1_gnn_b_conv1", "L1_gnn_b_lin1"]
_TURNED = ["L0_gnn_W2", "L1_gnn_W_conv0", "L1_gnn_W_lin0", "L1_gnn_W_conv1", "L1_gnn_W_lin1"]


def kernel(**inputs):
    import numpy as np
    import concourse.bacc as bacc
    from concourse.bass_utils import run_bass_kernel_spmd

    arrays = {k: np.ascontiguousarray(inputs[k]) for k in _PLAIN}
    for k in _TURNED:
        arrays[k + "_T"] = np.ascontiguousarray(np.asarray(inputs[k]).T)
    pad = GROUPS * GROUP * P - EDGES
    for k in ("src", "dst"):
        v = np.pad(np.asarray(inputs[k]), (0, pad), mode="edge")
        arrays[k] = np.ascontiguousarray(v.reshape(GROUPS * GROUP, P).T)
    v = np.pad(np.asarray(inputs["edge_attr_32"]), ((0, pad), (0, 0)), mode="edge")
    arrays["edge"] = np.ascontiguousarray(v.reshape(GROUPS, GROUP, P, E).transpose(1, 3, 0, 2).reshape(GROUP * E, GROUPS * P))

    nc = bacc.Bacc("TRN2", target_bir_lowering=False, num_devices=1)
    args, maps = {}, {}
    for k, v in arrays.items():
        maps["in_" + k] = v
        args[k] = nc.dram_tensor("in_" + k, v.shape, mybir.dt.from_np(v.dtype), kind="ExternalInput").ap()
    out = nc.dram_tensor("out_0", (NODES, D), F32, kind="ExternalOutput").ap()
    build(nc, args, out)
    r = run_bass_kernel_spmd(nc, [maps], core_ids=[0])
    return r.results[0]["out_0"]
```

```python
from contextlib import ExitStack

import concourse.bass as bass
from concourse import mybir

F32 = mybir.dt.float32
BF16 = mybir.dt.bfloat16
I32 = mybir.dt.int32
ALU = mybir.AluOpType
ACT = mybir.ActivationFunctionType
AX = mybir.AxisListType

P = 128
BANK = 512

NODES = 6250
EDGES = 100000
D = 128
E = 32
HID = 256
EPS = 1e-5

NODE_TILES = -(-NODES // P)
LAST_ROWS = NODES - (NODE_TILES - 1) * P
BATCH = BANK // D
BATCHES = -(-NODE_TILES // BATCH)
assert NODE_TILES - (BATCHES - 1) * BATCH == 1

GROUP = 4
TILES = -(-EDGES // P)
GROUPS = -(-TILES // GROUP)
LAST_EDGES = EDGES - (TILES - 1) * P
WINDOW = 80
WINDOWS = -(-NODES // WINDOW)
NODE_COLS = NODES + WINDOW
assert WINDOWS * WINDOW <= NODE_COLS and NODE_TILES * P <= NODE_COLS

SUPER = 4
LAG = SUPER + 1
AHEAD = 3
WIDE = LAG + AHEAD + 1
RING = 5
NODE_BUF = NODE_TILES * D
assert NODE_BUF + RING * GROUP * D <= WIDE * GROUP * HID
EDGE_CHUNK = 4
EDGE_CHUNKS = -(-GROUPS // EDGE_CHUNK)
STAGE_BUF = 3
SETUP_BUF = STAGE_BUF + 4
ROUNDS = 3
SPANS = [(0, 1), (1, 3), (3, 7), (7, BATCHES)]
WOVEN = 4
SPAN_TILES = BATCH * max(j - i for i, j in SPANS)
NORM_LAG = 4
TABLE_SLOTS = (4, 1, 1)
COUNT, ONE = 0, 32


def tiles_of(g):
    return min(GROUP, TILES - g * GROUP)


def nodes_of(b):
    return min(BATCH, NODE_TILES - b * BATCH)


def edges_of(t):
    return P if t < TILES - 1 else LAST_EDGES


def stores_of(r):
    return [len(range(i, BATCHES, TABLE_SLOTS[r])) for i in range(TABLE_SLOTS[r])]


def beside(g, lag):
    b = g - 2 - lag
    return [b] if 0 <= b < BATCHES else []


def gathered():
    count, out = [0] * RING, []
    for n in range(ROUNDS * GROUPS):
        count[n % RING] += 16 * tiles_of(n % GROUPS)
        out.append(count[n % RING])
    return out


GATHERED = gathered()


def build(nc, a, out):
    with ExitStack() as ctx:
        def sb(name, shape, dt=F32):
            return ctx.enter_context(nc.sbuf_tensor(name, shape, dt))

        def ps(name, shape):
            return ctx.enter_context(nc.psum_tensor(name, shape, F32))

        def sem(name):
            return ctx.enter_context(nc.semaphore(name))

        table = [nc.dram_tensor("table_mlp", (NODES, HID), F32).ap(),
                 nc.dram_tensor("table_conv0", (NODES, D), F32).ap(),
                 nc.dram_tensor("table_conv1", (NODES, D), F32).ap()]

        x = sb("x", [P, NODE_BUF])
        hT = sb("hT", [P, NODE_TILES * P])
        acc = sb("acc", [P, 3, NODE_COLS])
        wide = sb("wide", [P, WIDE * GROUP * HID])
        hidden = wide[:, 0:NODE_BUF]
        ring = wide[:, NODE_BUF:NODE_BUF + RING * GROUP * D].rearrange("p (r q d) -> p r q d", r=RING, q=GROUP)
        act = [sb(f"act{i}", [P, GROUP * HID]) for i in range(2)]
        onehot = sb("onehot", [P, 2, GROUP, WINDOW])
        edge = sb("edge", [P, 2, EDGE_CHUNK * P])
        src_i = sb("src_i", [P, GROUPS * GROUP], I32)
        dst_f = sb("dst_f", [P, GROUPS * GROUP])
        dst_rel = sb("dst_rel", [P, GROUPS * GROUP])
        base_f = sb("base_f", [P, GROUPS])
        base_i = sb("base_i", [P, GROUPS], I32)
        span_i = sb("span_i", [P, 1], I32)
        window_lo = sb("window_lo", [P, 1])
        w1a = sb("w1a", [P, HID])
        w1b = sb("w1b", [P, GROUP, HID])
        b1 = sb("b1", [P, HID])
        wu = sb("wu", [P, 2, D])
        w2u = sb("w2u", [P, 2, D])
        bu2 = sb("bu2", [P, D])
        w_lin = [sb(f"w_lin{i}", [P, D]) for i in range(2)]
        w_conv = [sb(f"w_conv{i}", [P, D]) for i in range(2)]
        b_conv = sb("b_conv", [P, 2, D])
        g1 = sb("g1", [P, HID])
        be1 = sb("be1", [P, HID])
        gu = sb("gu", [P, D])
        beu = sb("beu", [P, D])
        ones = sb("ones", [P, P], BF16)
        ident = sb("ident", [P, P])
        iota = sb("iota", [P, WINDOW])
        centre = sb("centre", [P, 2, 9])
        sumsq = sb("sumsq", [P, 2, SUPER * GROUP])
        rstd = sb("rstd", [P, 2, SUPER * GROUP])
        newton = sb("newton", [P, max(SUPER * GROUP, SPAN_TILES)])
        guess = sb("guess", [P, max(SUPER * GROUP, SPAN_TILES)], I32)
        rcount = sb("rcount", [P, NODE_TILES])
        bn = sb("bn", [P, 2, BATCH, 6])
        mean_var = sb("mean_var", [P, 4, BATCH, 2])
        usq = sb("usq", [P, 2, BATCH])
        variance = sb("variance", [P, 2, 2 * BATCH])
        scale = sb("scale", [P, 4, 2 * BATCH])
        shift = sb("shift", [P, 4, BATCH])
        mean_var0 = sb("mean_var0", [P, NODE_TILES, 2])
        variance0 = sb("variance0", [P, NODE_TILES])
        scale0 = sb("scale0", [P, NODE_TILES])
        shift0 = sb("shift0", [P, NODE_TILES])
        bn0 = sb("bn0", [P, SPAN_TILES, 6])
        iota_i = sb("iota_i", [P, WINDOW], I32)
        late = wide[:, SETUP_BUF * GROUP * HID:]
        b_parts = late[:, 0:4 * D].rearrange("p (i d) -> p i d", i=4)
        w2T = late[:, 4 * D:4 * D + HID]
        b2 = late[:, 4 * D + HID:4 * D + HID + 1]
        dst_i = late[:, GROUP * HID:GROUP * HID + GROUPS * GROUP].bitcast(I32)
        lo_hi = act[0][:, 0:2 * GROUPS].rearrange("p (i g) -> p i g", i=2)
        span = act[0][:, 2 * GROUPS:3 * GROUPS]
        span_max = act[0][:, 3 * GROUPS:3 * GROUPS + 1]
        lo_hi_col = act[0][:, 3 * GROUPS + 1:3 * GROUPS + 5]
        lo_hi_bc = act[1][:, 0:4 * P].rearrange("p (i c) -> p i c", i=4)

        mm = ps("mm", [P, 4, BANK])
        seg = ps("seg", [P, 2, BANK])
        node = ps("node", [P, 2, BANK])

        s_w1 = sem("s_w1")
        s_w1b = sem("s_w1b")
        s_w = sem("s_w")
        s_idx = sem("s_idx")
        s_x = [sem(f"s_x{i}") for i in range(BATCHES)]
        s_edge = [sem(f"s_edge{i}") for i in range(2)]
        s_rows = [sem(f"s_rows{i}") for i in range(RING)]
        s_table = [[sem(f"s_table{r}_{i}") for i in range(n)] for r, n in enumerate(TABLE_SLOTS)]
        s_out = sem("s_out")
        s_pad = sem("s_pad")
        s_const = sem("s_const")
        s_zero = sem("s_zero")
        s_weights = sem("s_weights")
        s_joint = sem("s_joint")
        s_jointc = sem("s_jointc")
        s_lohi = sem("s_lohi")
        s_lohiT = sem("s_lohiT")
        s_lohic = sem("s_lohic")
        s_base = sem("s_base")
        s_windows = sem("s_windows")
        link_v = sem("link_v")
        s_scale = [sem(f"s_scale{i}") for i in range(2)]
        s_h = [sem(f"s_h{i}") for i in range(2)]
        s_tr = [sem(f"s_tr{i}") for i in range(2)]
        s_hT = [sem(f"s_hT{i}") for i in range(2)]
        s_sum = [sem(f"s_sum{i}") for i in range(2)]
        s_p = sem("s_p")
        s_pc = sem("s_pc")
        s_u = sem("s_u")
        s_usq = sem("s_usq")
        s_un = sem("s_un")
        s_ub = sem("s_ub")
        s_ug = sem("s_ug")
        s_rezero = sem("s_rezero")
        s_cnt = sem("s_cnt")
        s_ew = sem("s_ew")
        s_copy = sem("s_copy")
        s_square = sem("s_square")
        s_scaled = sem("s_scaled")
        s_biased = sem("s_biased")
        s_gelu = sem("s_gelu")
        s_onehot = [sem(f"s_onehot{r}") for r in range(ROUNDS)]
        s_seg = [sem(f"s_seg{r}") for r in range(ROUNDS)]
        s_flush = [sem(f"s_flush{r}") for r in range(ROUNDS)]
        g_hot = sem("g_hot")
        g_seg = sem("g_seg")
        s_own = [sem(f"s_own{i}") for i in range(2)]
        s_ownc = [sem(f"s_ownc{i}") for i in range(2)]
        s_conv = [sem(f"s_conv{i}") for i in range(2)]
        s_res = [sem(f"s_res{i}") for i in range(2)]
        s_hid = sem("s_hid")
        s_hidT = sem("s_hidT")
        s_hidTc = sem("s_hidTc")

        def table_rows(t, b):
            r0 = b * BATCH * P
            if b == BATCHES - 1:
                return t[r0:NODES, :]
            return t[r0:r0 + BATCH * P, :].rearrange("(t p) d -> p t d", p=P)

        def stored(v, b):
            return v[0:LAST_ROWS, :] if b == BATCHES - 1 else v.rearrange("p (t d) -> p t d", t=BATCH)

        def batch(t, b):
            return t[:, b * BANK:b * BANK + nodes_of(b) * D]

        def tile(t, j):
            return t[:, j * P:(j + 1) * P]

        def tiles(v, n):
            return v.rearrange("p (t d) -> p t d", t=n)

        def mlp_buf(g):
            i = g % WIDE * GROUP * HID
            return wide[:, i:i + GROUP * HID]

        def staged(b):
            i = (STAGE_BUF + b % 4) * GROUP * HID
            return wide[:, i:i + GROUP * HID]

        def edge_banks(g):
            return slice(2, 4) if g % 2 == 0 else slice(0, 2)

        def phase0_h(b):
            i = b // 2 % 2 * BANK
            return act[b % 2][:, i:i + nodes_of(b) * D]

        def row(name):
            return a[name].rearrange("(a n) -> a n", a=1)

        first_weights = [(w1a[:, :], a["L0_gnn_W1"][0:D, :]), (b1[:, :], a["L0_gnn_b1"].partition_broadcast(P))]
        edge_weights = [(w1b[E * q:E * q + E, q, :], a["L0_gnn_W1"][D:D + E, :]) for q in range(GROUP)]
        weight_loads = [(v[:, :], a["L0_gnn_" + k].partition_broadcast(P))
                         for v, k in ((g1, "g1"), (be1, "be1"), (gu, "gu"), (beu, "beu"))]
        weight_loads += [(wu[:, :, :], a["L0_gnn_Wu"].rearrange("(h p) n -> p h n", p=P)), (bu2[ONE:ONE + 1, :], row("L0_gnn_bu")),
                         (w2T, a["L0_gnn_W2_T"]), (b2, a["L0_gnn_b2"].rearrange("(p a) -> p a", a=1))]
        weight_loads += [(w[i][:, :], a[f"L1_gnn_W_{k}{i}_T"]) for k, w in (("lin", w_lin), ("conv", w_conv)) for i in range(2)]
        weight_loads += [(b_parts[:, i, :], a["L1_gnn_b_" + k].partition_broadcast(P))
                         for i, k in enumerate(("conv0", "lin0", "conv1", "lin1"))]

        block = ctx.enter_context(nc.Block())

        @block.sync
        def _(sp):
            def load_x(b):
                v = batch(x, b)
                sp.dma_start(v[0:LAST_ROWS, :] if b == BATCHES - 1 else tiles(v, BATCH), table_rows(a["x"], b))\
                  .then_inc(s_x[b], 16)

            def load_weights(loads, done):
                for v, w in loads:
                    sp.dma_start(v, w).then_inc(done, 16)

            for b in range(4):
                load_x(b)
            sp.wait_ge(s_pad, 3)
            load_weights(first_weights, s_w1)
            for b in range(4, BATCHES):
                load_x(b)
            load_weights(edge_weights, s_w1b)
            sp.dma_start(dst_i, a["dst"]).then_inc(s_idx, 16)
            sp.dma_start(src_i[:, :], a["src"]).then_inc(s_idx, 16)

            def load_edges(c):
                if c >= 2:
                    sp.wait_ge(s_ew, EDGE_CHUNK * (c - 1))
                sp.dma_start(edge[:, c % 2, :], a["edge"][:, c * EDGE_CHUNK * P:(c + 1) * EDGE_CHUNK * P])\
                  .then_inc(s_edge[c % 2], 16)

            load_edges(0)
            load_edges(1)
            load_weights(weight_loads, s_w)
            for b in range(BATCHES):
                sp.wait_ge(s_pc, b + 1)
                v = staged(b)[:, 0:nodes_of(b) * HID]
                sp.dma_start(table_rows(table[0], b), stored(v, b)).then_inc(s_table[0][b % 4], 16)
            for c in range(2, EDGE_CHUNKS):
                load_edges(c)
            for b in range(BATCHES):
                sp.wait_ge(s_h[1], b + 1)
                sp.dma_start(table_rows(table[1], b), stored(batch(hidden, b), b)).then_inc(s_table[1][0], 16)
            for b in range(BATCHES):
                sp.wait_ge(s_hid, b + 1)
                sp.dma_start(table_rows(table[2], b), stored(batch(hidden, b), b)).then_inc(s_table[2][0], 16)
            for b in range(BATCHES):
                sp.wait_ge(s_res[1], b + 1)
                sp.dma_start(table_rows(out, b), stored(batch(x, b), b)).then_inc(s_out, 16)
            sp.wait_ge(s_out, 16 * BATCHES)

        @block.gpsimd
        def _(pool):
            pool.memset(w1b[:, :, :], 0.0).then_inc(s_pad, 1)
            pool.memset(bu2[:, :], 0.0).then_inc(s_pad, 1)
            pool.memset(tile(x, NODE_TILES - 1), 0.0).then_inc(s_pad, 1)
            pool.memset(ident[:, :], 0.0).then_inc(s_const, 1)
            pool.memset(ones[:, :], 1.0).then_inc(s_const, 1)
            pool.iota(iota_i[:, :], pattern=[[1, WINDOW]], base=0, channel_multiplier=0).then_inc(s_const, 1)
            pool.wait_ge(s_const, 3)
            pool.affine_select(out=ident[:, :], in_=ident[:, :], compare_op=ALU.not_equal, fill=1.0,
                               base=0, pattern=[[-1, P]], channel_multiplier=1).then_inc(s_const, 1)
            pool.memset(ones[:, ONE:ONE + 1], 0.0).then_inc(s_const, 1)

            pool.memset(acc[:, 2, :], 0.0).then_inc(s_zero, 1)
            pool.wait_ge(s_zero, 1)
            pool.memset(acc[ONE:ONE + 1, 2, :], 1.0).then_inc(s_zero, 1)
            pool.wait_ge(s_zero, 2)

            def add_to_x(phase, b, done):
                pool.wait_ge(done, b + 1)
                v = phase0_h(b) if phase == 0 else act[b % 2][:, 0:nodes_of(b) * D]
                pool.tensor_tensor(batch(x, b), batch(x, b), v, ALU.add).then_inc(s_sum[phase], 1)

            def add_beta(b):
                pool.wait_ge(s_un, b + 1)
                n = nodes_of(b)
                v = tiles(act[b % 2][:, 0:n * D], n)
                pool.tensor_tensor(v, v, beu[:, :].unsqueeze(1).to_broadcast([P, n, D]), ALU.add).then_inc(s_ub, 1)

            for b in range(BATCHES):
                to = NODE_COLS if b == BATCHES - 1 else (b + 1) * BANK
                pool.memset(acc[:, 0:2, b * BANK:to], 0.0).then_inc(s_zero, 1)
                add_to_x(0, b, s_h[0])
            pool.wait_ge(s_idx, 32)
            for r in range(ROUNDS):
                if r == 1:
                    for b in range(BATCHES + 2):
                        if b < BATCHES:
                            pool.wait_ge(s_u, b + 1)
                            to = NODE_COLS if b == BATCHES - 1 else (b + 1) * BANK
                            pool.memset(acc[:, 0:2, b * BANK:to], 0.0).then_inc(s_rezero, 1)
                        if 0 <= b - 1 < BATCHES:
                            add_beta(b - 1)
                        if b >= 2:
                            add_to_x(1, b - 2, s_ug)
                for s, n in zip(s_table[r], stores_of(r)):
                    pool.wait_ge(s, 16 * n)
                for g in range(GROUPS):
                    n = r * GROUPS + g
                    if r == 0:
                        pool.wait_ge(s_copy, g + 1)
                    elif g >= RING:
                        pool.wait_ge(s_seg[r], g - RING + 1)
                    for q in range(tiles_of(g)):
                        t = g * GROUP + q
                        index = bass.IndirectOffsetOnAxis(ap=src_i[:, t:t + 1], axis=0)
                        if r == 0:
                            ins = pool.indirect_dma_start(mlp_buf(g)[:, q * HID:(q + 1) * HID], None, table[r], index,
                                                          compute_op=ALU.add)
                        else:
                            ins = pool.indirect_dma_start(ring[:, n % RING, q, :], None, table[r], index)
                        ins.then_inc(s_rows[n % RING], 16)

        @block.tensor
        def _(pe):
            def transposes(phase, b):
                pe.wait_ge(s_h[phase], b + 1)
                if b >= 2:
                    pe.wait_ge(s_hT[phase], b - 1)
                v = phase0_h(b) if phase == 0 else batch(hidden, b)
                for j in range(nodes_of(b)):
                    last = pe.transpose(seg[:, b % 2, j * P:(j + 1) * P], tile(v, j), ident[:, :])
                last.then_inc(s_tr[phase], 1)

            def mlp_table(b):
                pe.wait_ge(s_hT[0], b + 1)
                if b >= 2:
                    pe.wait_ge(s_pc, b - 1)
                for j in range(nodes_of(b)):
                    last = pe.matmul(mm[:, 2 * (b % 2) + j // 2, (j % 2) * HID:(j % 2 + 1) * HID],
                                     tile(hT, b * BATCH + j), w1a[:, :], start=True, stop=True)
                last.then_inc(s_p, 1)

            def edge_part(g):
                c = g // EDGE_CHUNK
                pe.wait_ge(s_edge[c % 2], 16 * (c // 2 + 1))
                if g >= 2:
                    pe.wait_ge(s_copy, g - 1)
                col = (g % EDGE_CHUNK) * P
                for q in range(tiles_of(g)):
                    last = pe.matmul(mm[:, edge_banks(g).start + q // 2, (q % 2) * HID:(q % 2 + 1) * HID],
                                     edge[:, c % 2, col:col + P], w1b[:, q, :], start=True, stop=True)
                last.then_inc(s_ew, 1)

            pe.wait_ge(s_const, 4)
            for b in range(BATCHES + 1):
                if b < BATCHES:
                    transposes(0, b)
                if b == 1:
                    pe.wait_ge(s_weights, 1)
                if b >= 1:
                    mlp_table(b - 1)
            pe.wait_ge(s_weights, 2)
            pe.wait_ge(s_pc, BATCHES - 1)
            edge_part(0)
            pe.wait_ge(s_pc, BATCHES)
            edge_part(1)
            edge_part(2)
            pe.wait_ge(s_weights, 3)
            for h in range(2):
                pe.matmul(node[:, 0, h * D:(h + 1) * D], w2T[:, h * D:(h + 1) * D], wu[:, 1, :], start=True, stop=True)
            pe.matmul(node[0:1, 0, 2 * D:3 * D], b2, wu[:, 1, :], start=True, stop=True).then_inc(s_joint, 1)

            half = GROUPS // 2
            pe.wait_ge(s_lohi, 1)
            for i in range(4):
                last = pe.transpose(node[0:half, 1, i * P:(i + 1) * P],
                                    lo_hi[:, i // 2, (i % 2) * half:(i % 2 + 1) * half], ident[:, :])
            last.then_inc(s_lohiT, 1)
            pe.wait_ge(s_lohic, 1)
            for i in range(4):
                last = pe.matmul(node[:, 0, i * half:(i + 1) * half], lo_hi_bc[0:half, i, :],
                                 ident[0:half, 0:half], start=True, stop=True)
            last.then_inc(s_base, 1)

            def window_sums(r, g):
                n, nt = r * GROUPS + g, tiles_of(g)
                for h in ([2, 0, 1] if r == 0 else [0]):
                    for q in range(nt):
                        k = edges_of(g * GROUP + q)
                        hot = onehot[0:k, g % 2, q, :]
                        if h == 2:
                            v, hot = ones[0:k, :], hot.bitcast(BF16).rearrange("p (w half) -> p w half", half=2)[:, :, 1]
                        elif r == 0:
                            v = act[g % 2][0:k, q * HID + h * D:q * HID + (h + 1) * D]
                        else:
                            v = ring[0:k, n % RING, q, :]
                        last = pe.matmul(seg[:, g % 2, h * WINDOW:(h + 1) * WINDOW], v,
                                         hot, start=(q == 0), stop=(q == nt - 1))
                return last

            def segment(r, g, general):
                n = r * GROUPS + g
                if g >= 2:
                    pe.wait_ge(s_flush[r], g - 1)
                if r == 0:
                    pe.wait_ge(s_gelu, g + 1)
                else:
                    pe.wait_ge(s_rows[n % RING], GATHERED[n])
                if not general:
                    pe.wait_ge(s_onehot[r], g + 1)
                    window_sums(r, g).then_inc(s_seg[r], 1)
                    return
                with pe.Fori(0, WINDOWS):
                    pe.wait_ge(g_hot, 1)
                    pe.sem_clear(g_hot)
                    window_sums(r, g).then_inc(g_seg, 1)
                pe.drain().then_inc(s_seg[r], 1)

            def update(b):
                if b >= 4:
                    pe.wait_ge(s_un, b - 3)
                for j in range(nodes_of(b)):
                    o, t = mm[:, b % 4, j * D:(j + 1) * D], b * BATCH + j
                    pe.matmul(o, tile(hT, t), wu[:, 0, :], start=True, stop=False)
                    pe.matmul(o, tile(acc[:, 0, :], t), w2u[:, 0, :], start=False, stop=False)
                    pe.matmul(o, tile(acc[:, 1, :], t), w2u[:, 1, :], start=False, stop=False)
                    last = pe.matmul(o, tile(acc[:, 2, :], t), bu2[:, :], start=False, stop=True)
                last.then_inc(s_u, 1)

            def node_products(bank, b, lhs, rhs, done):
                for j in range(nodes_of(b)):
                    last = pe.matmul(mm[:, bank, j * D:(j + 1) * D], tile(lhs, b * BATCH + j), rhs, start=True, stop=True)
                last.then_inc(done, 1)

            def own_part(i, b):
                if i == 0:
                    if b >= 4:
                        pe.wait_ge(s_ownc[0], b - 3)
                    node_products(b % 4, b, hT, w_lin[0][:, :], s_own[0])
                else:
                    pe.wait_ge(s_hidTc, b + 1)
                    if b >= 2:
                        pe.wait_ge(s_ownc[1], b - 1)
                    node_products(2 + b % 2, b, hT, w_lin[1][:, :], s_own[1])

            def hidden_transposes(b):
                if b == 0:
                    pe.wait_ge(s_hid, BATCHES)
                if b >= 2:
                    pe.wait_ge(s_hidTc, b - 1)
                for j in range(nodes_of(b)):
                    last = pe.transpose(mm[:, b % 2, j * P:(j + 1) * P], tile(hidden, b * BATCH + j), ident[:, :])
                last.then_inc(s_hidT, 1)

            def mean_parts(i):
                pe.wait_ge(s_flush[i + 1], GROUPS)
                pe.wait_ge(s_ownc[i], BATCHES)
                for b in range(BATCHES):
                    if b >= 4:
                        pe.wait_ge(s_res[i], b - 3)
                    node_products(b % 4, b, acc[:, i, :], w_conv[i][:, :], s_conv[i])

            def rounds(general):
                for i in range(3, GROUPS + LAG + 1 + AHEAD):
                    if i < GROUPS:
                        edge_part(i)
                    if i - AHEAD > LAG:
                        segment(0, i - AHEAD - LAG - 1, general)
                pe.wait_ge(s_flush[0], GROUPS)
                pe.wait_ge(s_jointc, 1)
                for b in range(BATCHES + NORM_LAG + 3):
                    if b < BATCHES:
                        update(b)
                    if b >= NORM_LAG + 3:
                        transposes(1, b - NORM_LAG - 3)
                for j in range(NODE_TILES):
                    last = pe.matmul(node[:, 0, j:j + 1], tile(acc[:, 2, :], j), ident[:, COUNT:COUNT + 1], start=True, stop=True)
                last.then_inc(s_cnt, 1)
                pe.wait_ge(s_hT[1], BATCHES)
                for g in range(GROUPS):
                    segment(1, g, general)
                    for b in beside(g, 0):
                        own_part(0, b)
                mean_parts(0)
                for g in range(GROUPS):
                    segment(2, g, general)
                    for b in beside(g, 0):
                        hidden_transposes(b)
                    for b in beside(g, 1):
                        own_part(1, b)
                mean_parts(1)

            pe.wait_ge(s_windows, 1)
            widest = pe.value_load(span_i[0:1, 0:1], min_val=0, max_val=NODES)
            with pe.If(widest >= WINDOW):
                rounds(True)
            with pe.Else():
                rounds(False)

        @block.scalar
        def _(ac):
            def relu_norm(phase, b):
                of_span = [i for i, (_, last) in enumerate(SPANS) if b < last][0]
                ac.wait_ge(s_scale[phase], (of_span if phase == 0 else b) + 1)
                if phase == 0 and b >= 4:
                    ac.wait_ge(s_tr[0], b - 3)
                    ac.wait_ge(s_sum[0], b - 3)
                o = phase0_h(b) if phase == 0 else batch(hidden, b)
                slot = (b + NORM_LAG) % 4
                for j in range(nodes_of(b)):
                    t = b * BATCH + j
                    if phase == 0:
                        by, plus = scale0[:, t:t + 1], shift0[:, t:t + 1]
                    else:
                        by, plus = scale[:, slot, BATCH + j:BATCH + j + 1], shift[:, slot, j:j + 1]
                    last = ac.activation(tile(o, j), tile(x, t), ACT.Relu, bias=plus, scale=by)
                last.then_inc(s_h[phase], 1)

            def copy_hT(phase, b):
                ac.wait_ge(s_tr[phase], b + 1)
                ac.activation(batch(hT, b), seg[:, b % 2, 0:nodes_of(b) * P], ACT.Copy).then_inc(s_hT[phase], 1)

            for b in range(BATCHES + 1):
                if b < BATCHES:
                    relu_norm(0, b)
                if b >= 1:
                    copy_hT(0, b - 1)

            def copy_edge_part(g):
                k = tiles_of(g) * HID
                ac.wait_ge(s_ew, g + 1)
                if g == STAGE_BUF:
                    for s, n in zip(s_table[0], stores_of(0)):
                        ac.wait_ge(s, 16 * n)
                if g == SETUP_BUF:
                    ac.wait_ge(s_windows, 1)
                if g >= WIDE:
                    ac.wait_ge(s_gelu, g - WIDE + 1)
                ac.activation(mlp_buf(g)[:, 0:k], mm[:, edge_banks(g), :].rearrange("p b c -> p (b c)")[:, 0:k], ACT.Copy)\
                  .then_inc(s_copy, 1)

            def squares(g):
                if g == 0:
                    ac.wait_ge(s_windows, 1)
                ac.wait_ge(s_rows[g % RING], GATHERED[g])
                if g >= 1:
                    ac.wait_ge(s_square, g)
                if g % SUPER == 0 and g >= 2 * SUPER:
                    ac.wait_ge(s_scaled, g - 2 * SUPER + 1)
                for q in range(tiles_of(g)):
                    t = (g % SUPER) * GROUP + q
                    last = ac.activation(node[:, q // 2, (q % 2) * HID:(q % 2 + 1) * HID], mlp_buf(g)[:, q * HID:(q + 1) * HID],
                                         ACT.Square, accum_out=sumsq[:, g // SUPER % 2, t:t + 1])
                last.then_inc(s_square, 1)

            def gelu(g):
                k = tiles_of(g) * HID
                ac.wait_ge(s_biased, g + 1)
                if g >= 2:
                    ac.wait_ge(s_seg[0], g - 1)
                ac.activation(act[g % 2][:, 0:k], mlp_buf(g)[:, 0:k], ACT.Gelu).then_inc(s_gelu, 1)

            ac.wait_ge(s_sum[0], BATCHES)
            for g in range(AHEAD):
                copy_edge_part(g)
            for g in range(GROUPS + LAG):
                if g + AHEAD < GROUPS:
                    copy_edge_part(g + AHEAD)
                if g < GROUPS:
                    squares(g)
                if g >= LAG:
                    gelu(g - LAG)

            ac.wait_ge(s_seg[0], GROUPS)
            for i in range(BATCHES + NORM_LAG + 2):
                if i < BATCHES:
                    ac.wait_ge(s_u, i + 1)
                    if i >= 1:
                        ac.wait_ge(s_usq, i)
                    if i >= 2:
                        ac.wait_ge(s_un, i - 1)
                    for j in range(nodes_of(i)):
                        last = ac.activation(act[0][:, (4 + j) * D:(5 + j) * D], mm[:, i % 4, j * D:(j + 1) * D], ACT.Square,
                                             accum_out=usq[:, i % 2, j:j + 1])
                    last.then_inc(s_usq, 1)
                b = i - 2
                if 0 <= b < BATCHES:
                    v = act[b % 2][:, 0:nodes_of(b) * D]
                    ac.wait_ge(s_ub, b + 1)
                    ac.activation(v, v, ACT.Gelu).then_inc(s_ug, 1)
                if 0 <= i - NORM_LAG - 1 < BATCHES:
                    relu_norm(1, i - NORM_LAG - 1)
                if 0 <= i - NORM_LAG - 2 < BATCHES:
                    copy_hT(1, i - NORM_LAG - 2)

            for b in range(BATCHES):
                ac.wait_ge(s_res[0], b + 1)
                ac.activation(batch(hidden, b), batch(hidden, b), ACT.Relu).then_inc(s_hid, 1)
            for b in range(BATCHES):
                ac.wait_ge(s_hidT, b + 1)
                ac.activation(batch(hT, b), mm[:, b % 2, 0:nodes_of(b) * P], ACT.Copy).then_inc(s_hidTc, 1)

        @block.vector
        def _(ve):
            linked = [0]

            def link(ins):
                linked[0] += 1
                ins.then_inc(link_v, 1)
                ve.wait_ge(link_v, linked[0])

            def tt(o, i0, i1, op):
                return ve.tensor_tensor(o, i0, i1, op)

            def ts(o, i0, s1, s2, op0, op1=None):
                if op1 is None:
                    return ve.tensor_scalar(o, i0, s1, None, op0)
                return ve.tensor_scalar(o, i0, s1, s2, op0, op1)

            def stt(o, i0, s, i1, op0, op1):
                return ve.scalar_tensor_tensor(out=o, in0=i0, scalar=s, in1=i1, op0=op0, op1=op1)

            class Chain:

                def __init__(self, result=0):
                    self.steps, self.result = [], result

                def add(self, make):
                    def step():
                        self.wait()
                        linked[0] += 1
                        make().then_inc(link_v, 1)
                        self.result = linked[0]
                    self.steps.append(step)

                def wait(self):
                    if self.result:
                        ve.wait_ge(link_v, self.result)

            def weave(chain, others):
                others = list(others)
                for s in chain.steps:
                    s()
                    if others:
                        others.pop(0)()
                for o in others:
                    o()
                chain.wait()

            def inverse_root(chain, y, v):
                n = v.shape[1]
                gi, t = guess[:, 0:n], newton[:, 0:n]
                chain.add(lambda: ts(gi, v.bitcast(I32), 1, None, ALU.logical_shift_right))
                chain.add(lambda: ts(gi, gi, -1.0, float(0x5F3759DF), ALU.mult, ALU.add))
                for g in (gi.bitcast(F32), y, y):
                    chain.add(lambda g=g: tt(t, g, g, ALU.mult))
                    chain.add(lambda g=g: stt(t, t, -0.5, v, ALU.mult, ALU.mult))
                    chain.add(lambda g=g: stt(y, t, 1.5, g, ALU.add, ALU.mult))

            def statistics(t0, t1, stats_of, to, ready):
                last = [0]

                def stats(t):
                    if t % BATCH == 0:
                        ready(t // BATCH)
                    ins = ve.bn_stats(stats_of(t), tile(x, t))
                    if t == t1 - 1:
                        linked[0] += 1
                        last[0] = linked[0]
                        ins.then_inc(link_v, 1)

                def aggregate(t):
                    if t == t0:
                        ve.wait_ge(link_v, last[0])
                    ins = ve.bn_aggr(to(t), stats_of(t))
                    if t == t1 - 1:
                        linked[0] += 1
                        ins.then_inc(link_v, 1)
                        aggregated[0] = linked[0]

                return [lambda t=t: stats(t) for t in range(t0, t1)], [lambda t=t: aggregate(t) for t in range(t0, t1)]

            aggregated = [0]

            def norm_shift(b, slot, first):
                n = nodes_of(b)
                return stt(shift[:, slot, 0:n], mean_var[:, b % 4, 0:n, 0], -1.0, scale[:, slot, first:first + n],
                           ALU.mult, ALU.mult)

            def centre_rows(slot, views, width):
                n = len(views)
                def sums():
                    for i, v in enumerate(views):
                        last = ve.tensor_reduce(centre[:, 0, slot + i:slot + i + 1], v, AX.X, ALU.add)
                    link(last)
                def means():
                    link(ts(centre[:, 1, slot:slot + n], centre[:, 0, slot:slot + n], -1.0 / width, None, ALU.mult))
                def take():
                    for i, v in enumerate(views):
                        last = ts(v, v, centre[:, 1, slot + i:slot + i + 1], None, ALU.add)
                    last.then_inc(s_weights, 1)
                return [sums, means, take]

            def table_weights():
                ve.wait_ge(s_w1, 16 * len(first_weights))
                for step in centre_rows(0, [w1a[:, :], b1[:, :]], HID):
                    step()
                ve.wait_ge(s_weights, 1)

            def update_weights():
                ve.wait_ge(s_w, 16 * len(weight_loads))
                ts(g1[:, :], g1[:, :], float(HID) ** 0.5, None, ALU.mult)
                for step in centre_rows(6, [wu[:, 0, :], wu[:, 1, :], bu2[:, :]], D):
                    step()
                ve.wait_ge(s_weights, 3)

            def table_copy(b):
                out = []
                n = nodes_of(b)
                def one(i):
                    if i == 0:
                        ve.wait_ge(s_p, b + 1)
                        if b >= 4:
                            ve.wait_ge(s_table[0][b % 4], 16 * (b // 4))
                    k = min(2, n - i)
                    o = tiles(staged(b)[:, i * HID:(i + k) * HID], k)
                    ins = tt(o, tiles(mm[:, 2 * (b % 2) + i // 2, 0:k * HID], k),
                             b1[:, :].unsqueeze(1).to_broadcast([P, k, HID]), ALU.add)
                    if i + k == n:
                        ins.then_inc(s_pc, 1)
                return [lambda i=i: one(i) for i in range(0, n, 2)]

            def span_statistics(i):
                t0, t1 = SPANS[i][0] * BATCH, min(SPANS[i][1] * BATCH, NODE_TILES)
                return statistics(t0, t1, lambda t: bn0[:, t - t0, :], lambda t: mean_var0[:, t, :],
                                  lambda b: ve.wait_ge(s_x[b], 16))

            for steps in span_statistics(0):
                for s in steps:
                    s()
            for i, (b0, b_end) in enumerate(SPANS):
                t0, t1 = b0 * BATCH, min(b_end * BATCH, NODE_TILES)
                last = i == len(SPANS) - 1
                if i == 1:
                    table_weights()
                chain, v = Chain(aggregated[0]), variance0[:, t0:t1]
                chain.add(lambda: ts(v, mean_var0[:, t0:t1, 1], EPS, None, ALU.add))
                inverse_root(chain, scale0[:, t0:t1], v)
                weave(chain, sum([table_copy(b) for b in range(2, WOVEN)], []) if last else [])
                stt(shift0[:, t0:t1], mean_var0[:, t0:t1, 0], -1.0, scale0[:, t0:t1], ALU.mult, ALU.mult).then_inc(s_scale[0], 1)
                if not last:
                    stats, aggregates = span_statistics(i + 1)
                    if i + 1 == len(SPANS) - 1:
                        middle = len(stats) // 2
                        stats = stats[:middle] + table_copy(0) + stats[middle:] + table_copy(1)
                    for s in stats + aggregates:
                        s()
            edge_steps = centre_rows(2, [w1b[:, q, :] for q in range(GROUP)], HID)
            for b in range(WOVEN, BATCHES):
                for s in table_copy(b):
                    s()
                if edge_steps:
                    if b == WOVEN:
                        ve.wait_ge(s_w1b, 16 * len(edge_weights))
                    edge_steps.pop(0)()
            for s in edge_steps:
                s()

            ve.wait_ge(s_idx, 32)
            link(ve.tensor_copy(dst_f[:, :], dst_i))
            ve.wait_ge(s_sum[0], BATCHES)
            by_group = dst_f[:, :].rearrange("p (g q) -> p g q", q=GROUP)
            ve.tensor_reduce(lo_hi[:, 0, :], by_group, AX.X, ALU.min)
            ve.tensor_reduce(lo_hi[:, 1, :], by_group, AX.X, ALU.max).then_inc(s_lohi, 1)
            update_weights()
            for i in range(2):
                tt(b_conv[:, i, :], b_parts[:, 2 * i, :], b_parts[:, 2 * i + 1, :], ALU.add)
            ve.wait_ge(s_joint, 1)
            ve.tensor_copy(w2u[:, :, :], tiles(node[:, 0, 0:2 * D], 2))
            ve.tensor_copy(bu2[COUNT:COUNT + 1, :], node[COUNT:COUNT + 1, 0, 2 * D:3 * D]).then_inc(s_jointc, 1)
            ve.wait_ge(s_lohiT, 1)
            half = GROUPS // 2
            v = node[0:half, 1, :].rearrange("p (i c) -> p i c", i=4)
            ve.tensor_reduce(lo_hi_col[0:half, 0:2], v[:, 0:2, :], AX.X, ALU.min)
            link(ve.tensor_reduce(lo_hi_col[0:half, 2:4], v[:, 2:4, :], AX.X, ALU.max))
            ve.tensor_copy(lo_hi_bc[0:half, :, :], lo_hi_col[0:half, :].unsqueeze(2).to_broadcast([half, 4, P]))\
              .then_inc(s_lohic, 1)
            ve.wait_ge(s_base, 1)
            link(ve.tensor_copy(base_f[:, :], node[:, 0, 0:GROUPS]))
            ve.tensor_copy(base_i[:, :], base_f[:, :])
            link(tt(span, node[:, 0, GROUPS:2 * GROUPS], base_f[:, :], ALU.subtract))
            link(ve.tensor_reduce(span_max, span, AX.X, ALU.max))
            ve.tensor_copy(span_i[:, :], span_max)
            ve.wait_ge(s_const, 5)
            ve.tensor_copy(iota[:, :], iota_i[:, :])
            tt(dst_rel[:, :].rearrange("p (g q) -> p g q", q=GROUP), by_group,
               base_f[:, :].unsqueeze(2).to_broadcast([P, GROUPS, GROUP]), ALU.subtract).then_inc(s_windows, 1)
            ve.wait_ge(s_windows, 1)

            def hot(r, g, general):
                if general:
                    return
                if g >= 2:
                    ve.wait_ge(s_seg[r], g - 1)
                n, t = tiles_of(g), g * GROUP
                tt(onehot[:, g % 2, 0:n, :], iota[:, :].unsqueeze(1).to_broadcast([P, n, WINDOW]),
                   dst_rel[:, t:t + n].unsqueeze(2).to_broadcast([P, n, WINDOW]), ALU.is_equal).then_inc(s_onehot[r], 1)

            def add_window(r, g, start):
                parts = slice(0, 3) if r == 0 else slice(r - 1, r)
                n = 3 if r == 0 else 1
                o = acc[:, parts, bass.ds(start, WINDOW)]
                return tt(o, o, seg[:, g % 2, 0:n * WINDOW].rearrange("p (h w) -> p h w", h=n), ALU.add)

            def flush(r, g, general):
                if not general:
                    start = ve.value_load(base_i[0:1, g:g + 1], min_val=0, max_val=NODES - 1)
                    ve.wait_ge(s_seg[r], g + 1)
                    if g >= 1:
                        ve.wait_ge(s_flush[r], g)
                    add_window(r, g, start).then_inc(s_flush[r], 1)
                    return
                ve.memset(window_lo[:, :], 0.0)
                with ve.Fori(0, WINDOWS) as w:
                    ve.drain()
                    for q in range(tiles_of(g)):
                        t = g * GROUP + q
                        last = ts(onehot[:, g % 2, q, :], iota[:, :], window_lo[:, 0:1], dst_f[:, t:t + 1],
                                  ALU.add, ALU.is_equal)
                    last.then_inc(g_hot, 1)
                    ve.wait_ge(g_seg, 1)
                    ve.sem_clear(g_seg)
                    add_window(r, g, w * WINDOW)
                    ts(window_lo[:, :], window_lo[:, :], float(WINDOW), None, ALU.add)
                ve.drain().then_inc(s_flush[r], 1)

            def mlp_round(general):
                inverted = {}

                def invert(i):
                    first = i * SUPER
                    last = min(first + SUPER, GROUPS) - 1
                    n = (last - first) * GROUP + tiles_of(last)
                    v = sumsq[:, i % 2, 0:n]
                    chain = inverted[i] = Chain()

                    def begin():
                        ve.wait_ge(s_square, last + 1)
                        return ts(v, v, HID * EPS, None, ALU.add)

                    chain.add(begin)
                    inverse_root(chain, rstd[:, i % 2, 0:n], v)
                    return chain

                def normalise(g):
                    k = tiles_of(g)

                    def scaled(q):
                        if q == 0:
                            inverted[g // SUPER].wait()
                        v, t = mlp_buf(g)[:, q * HID:(q + 1) * HID], (g % SUPER) * GROUP + q
                        ins = stt(v, v, rstd[:, g // SUPER % 2, t:t + 1], g1[:, :], ALU.mult, ALU.mult)
                        if q == k - 1:
                            ins.then_inc(s_scaled, 1)

                    def biased():
                        ve.wait_ge(s_scaled, g + 1)
                        v = tiles(mlp_buf(g)[:, 0:k * HID], k)
                        tt(v, v, be1[:, :].unsqueeze(1).to_broadcast([P, k, HID]), ALU.add).then_inc(s_biased, 1)

                    return [lambda q=q: scaled(q) for q in range(k)], biased

                for i in range(GROUPS + LAG + 2):
                    others, g = [], i - LAG
                    if 0 <= g < GROUPS:
                        scaled, biased = normalise(g)
                        others = scaled + [lambda: hot(0, g, general), biased]
                    if g >= 2:
                        others.append(lambda: flush(0, g - 2, general))
                    if i % SUPER == 0 and 0 < i <= GROUPS or i == GROUPS:
                        first = others.pop(0) if others else lambda: None
                        first()
                        weave(invert((i - 1) // SUPER), others)
                    else:
                        for o in others:
                            o()

            def node_update():
                inverted = {}

                def normalise_u(b):
                    n = nodes_of(b)
                    v = act[b % 2][:, 0:n * D]

                    def scaled(j):
                        if j == 0 and b >= 2:
                            ve.wait_ge(s_sum[1], b - 1)
                        ins = stt(tile(v, j), mm[:, b % 4, j * D:(j + 1) * D], scale[:, b % 4, j:j + 1], gu[:, :], ALU.mult, ALU.mult)
                        if j == n - 1:
                            ins.then_inc(s_un, 1)

                    return [lambda j=j: scaled(j) for j in range(n)]

                link(ve.memset(variance[:, :, :], 1.0))
                aggregated[0] = 0
                for i in range(BATCHES + NORM_LAG):
                    b = i - NORM_LAG
                    chain = Chain(aggregated[0])
                    v = variance[:, i % 2, :]
                    others = normalise_u(i - 1) if 1 <= i <= BATCHES else []
                    if 0 <= b + 1 < BATCHES:
                        t0 = (b + 1) * BATCH
                        stats, aggregates = statistics(
                            t0, t0 + nodes_of(b + 1), lambda t: bn[:, t // BATCH % 2, t % BATCH, :],
                            lambda t: mean_var[:, t // BATCH % 4, t % BATCH, :],
                            lambda k: ve.wait_ge(s_sum[1], k + 1))
                        others += stats + aggregates
                    if b >= 0:
                        chain.add(lambda: ts(v[:, BATCH:BATCH + nodes_of(b)], mean_var[:, b % 4, 0:nodes_of(b), 1], EPS, None, ALU.add))
                    if i < BATCHES:
                        ve.wait_ge(s_usq, i + 1)
                        chain.add(lambda: ts(v[:, 0:nodes_of(i)], usq[:, i % 2, 0:nodes_of(i)], 1.0 / D, EPS, ALU.mult, ALU.add))
                    if b >= 4:
                        ve.wait_ge(s_h[1], b - 3)
                    inverse_root(chain, scale[:, i % 4, :], v)
                    weave(chain, others)
                    if b >= 0:
                        norm_shift(b, i % 4, BATCH).then_inc(s_scale[1], 1)

            def own_copy(i, b):
                n = nodes_of(b)
                ve.wait_ge(s_own[i], b + 1)
                bias = b_conv[:, i, :].unsqueeze(1).to_broadcast([P, n, D])
                if i == 0:
                    if b == 0:
                        for s, k in zip(s_table[1], stores_of(1)):
                            ve.wait_ge(s, 16 * k)
                    tt(tiles(batch(hidden, b), n), tiles(mm[:, b % 4, 0:n * D], n), bias, ALU.add).then_inc(s_ownc[0], 1)
                else:
                    v = batch(x, b)
                    link(tt(v, v, mm[:, 2 + b % 2, 0:n * D], ALU.add))
                    tt(tiles(v, n), tiles(v, n), bias, ALU.add).then_inc(s_ownc[1], 1)

            def conv_round(r, general):
                if r == 1:
                    ve.wait_ge(s_rezero, BATCHES)
                for g in range(GROUPS + 1):
                    if g < GROUPS:
                        hot(r, g, general)
                    if g >= 1:
                        flush(r, g - 1, general)
                        for b in beside(g - 1, r - 1):
                            own_copy(r - 1, b)
                    if r == 1 and g == 1:
                        ve.wait_ge(s_cnt, 1)
                        link(ts(rcount[:, :], node[:, 0, 0:NODE_TILES], 1.0, None, ALU.max))
                        link(ve.reciprocal(rcount[:, :], rcount[:, :]))

            def add_means(i):
                v = hidden if i == 0 else x
                ve.wait_ge(s_ownc[i], BATCHES)
                for b in range(BATCHES):
                    ve.wait_ge(s_conv[i], b + 1)
                    for j in range(nodes_of(b)):
                        t = b * BATCH + j
                        last = stt(tile(v, t), mm[:, b % 4, j * D:(j + 1) * D], rcount[:, t:t + 1], tile(v, t), ALU.mult, ALU.add)
                    last.then_inc(s_res[i], 1)

            def rounds(general):
                mlp_round(general)
                node_update()
                conv_round(1, general)
                add_means(0)
                conv_round(2, general)
                add_means(1)

            ve.wait_ge(s_zero, 2 + BATCHES)
            widest = ve.value_load(span_i[0:1, 0:1], min_val=0, max_val=NODES)
            before = linked[0]
            with ve.If(widest >= WINDOW):
                rounds(True)
            linked[0] = before
            with ve.Else():
                rounds(False)


_PLAIN = ["x", "L0_gnn_W1", "L0_gnn_b1", "L0_gnn_g1", "L0_gnn_be1", "L0_gnn_b2", "L0_gnn_Wu", "L0_gnn_bu",
          "L0_gnn_gu", "L0_gnn_beu", "L1_gnn_b_conv0", "L1_gnn_b_lin0", "L1_gnn_b_conv1", "L1_gnn_b_lin1"]
_TURNED = ["L0_gnn_W2", "L1_gnn_W_conv0", "L1_gnn_W_lin0", "L1_gnn_W_conv1", "L1_gnn_W_lin1"]


def kernel(**inputs):
    import numpy as np
    import concourse.bacc as bacc
    from concourse.bass_utils import run_bass_kernel_spmd

    arrays = {k: np.ascontiguousarray(inputs[k]) for k in _PLAIN}
    for k in _TURNED:
        arrays[k + "_T"] = np.ascontiguousarray(np.asarray(inputs[k]).T)
    pad = GROUPS * GROUP * P - EDGES
    for k in ("src", "dst"):
        v = np.pad(np.asarray(inputs[k]), (0, pad), mode="edge")
        arrays[k] = np.ascontiguousarray(v.reshape(GROUPS * GROUP, P).T)
    v = np.pad(np.asarray(inputs["edge_attr_32"]), ((0, pad), (0, 0)), mode="edge")
    arrays["edge"] = np.ascontiguousarray(v.reshape(GROUPS, GROUP, P, E).transpose(1, 3, 0, 2).reshape(GROUP * E, GROUPS * P))

    nc = bacc.Bacc("TRN2", target_bir_lowering=False, num_devices=1)
    args, maps = {}, {}
    for k, v in arrays.items():
        maps["in_" + k] = v
        args[k] = nc.dram_tensor("in_" + k, v.shape, mybir.dt.from_np(v.dtype), kind="ExternalInput").ap()
    out = nc.dram_tensor("out_0", (NODES, D), F32, kind="ExternalOutput").ap()
    build(nc, args, out)
    r = run_bass_kernel_spmd(nc, [maps], core_ids=[0])
    return r.results[0]["out_0"]
```
